# Optimizing a Trainium2 kernel written in Bass

```python
import numpy as np
import jax
import jax.numpy as jnp

def _softmax(x, axis=-1):
    return jax.nn.softmax(x, axis=axis)

def _gelu(x):
    return jax.nn.gelu(x, approximate=True)

def _silu(x):
    return jax.nn.silu(x)

def _sigmoid(x):
    return jax.nn.sigmoid(x)

def _layernorm(x, axis=-1, eps=1e-05):
    m = jnp.mean(x, axis=axis, keepdims=True)
    v = jnp.var(x, axis=axis, keepdims=True)
    return (x - m) / jnp.sqrt(v + eps)

def _scatter_add(tgt, idx, src, axis=0):
    return tgt.at[idx].add(src)

def _segment_sum(src, seg, n):
    return jax.ops.segment_sum(src, seg, n)
kernel_name = 'mk_gnn_preln_d2_gnn_r64_512ac5'

def setup_inputs(seed: int=0):
    np.random.seed(seed)
    _w = jnp.asarray

    def _rec_inputs():
        import jax
        import jax.numpy as jnp
        _gk = jax.random.key(seed)
        x = -0.000202 + 1 * jax.random.normal(jax.random.fold_in(_gk, 1), (100000, 128), jnp.float32)
        src = jax.random.randint(jax.random.fold_in(_gk, 2), (25000,), 0, 100000, jnp.int32)
        dst = jax.random.randint(jax.random.fold_in(_gk, 3), (25000,), 0, 100000, jnp.int32)
        _o = jnp.argsort(dst, stable=True)
        src = src[_o]
        dst = dst[_o]
        edge_attr_128 = 2.93046e-05 + 1.00006 * jax.random.normal(jax.random.fold_in(_gk, 12), (25000, 128), jnp.float32)
        return (x, src, dst, edge_attr_128)
    x, src, dst, edge_attr_128 = _rec_inputs()

    def _L0_gnn_setup():
        import jax, jax.numpy as jnp
        import numpy as np
        N_NODES = 50000
        N_EDGES = 10000
        HID = 128
        LN_EPS = 1e-05

        def _layer_norm(h, gamma, beta):
            mu = jnp.mean(h, axis=-1, keepdims=True)
            var = jnp.mean(jnp.square(h - mu), axis=-1, keepdims=True)
            return (h - mu) * jax.lax.rsqrt(var + LN_EPS) * gamma + beta
        key = jax.random.key(seed)
        ks = jax.random.split(key, 8)
        x = jax.random.normal(ks[0], (N_NODES, HID), dtype=jnp.float32)
        edge_index = jax.random.randint(ks[1], (2, N_EDGES), 0, N_NODES, dtype=jnp.int64)
        edge_attr = jax.random.normal(ks[2], (N_EDGES, HID), dtype=jnp.float32)
        msg_W1 = jax.random.normal(ks[3], (3 * HID, HID), dtype=jnp.float32) / np.sqrt(3 * HID)
        msg_b1 = jnp.zeros((HID,), dtype=jnp.float32)
        msg_W2 = jax.random.normal(ks[4], (HID, HID), dtype=jnp.float32) / np.sqrt(HID)
        msg_b2 = jnp.zeros((HID,), dtype=jnp.float32)
        upd_W1 = jax.random.normal(ks[5], (2 * HID, HID), dtype=jnp.float32) / np.sqrt(2 * HID)
        upd_b1 = jnp.zeros((HID,), dtype=jnp.float32)
        upd_W2 = jax.random.normal(ks[6], (HID, HID), dtype=jnp.float32) / np.sqrt(HID)
        upd_b2 = jnp.zeros((HID,), dtype=jnp.float32)
        ln_gamma = jnp.ones((HID,), dtype=jnp.float32)
        ln_beta = jnp.zeros((HID,), dtype=jnp.float32)
        return {'x': x, 'edge_index': edge_index, 'edge_attr': edge_attr, 'msg_W1': msg_W1, 'msg_b1': msg_b1, 'msg_W2': msg_W2, 'msg_b2': msg_b2, 'upd_W1': upd_W1, 'upd_b1': upd_b1, 'upd_W2': upd_W2, 'upd_b2': upd_b2, 'ln_gamma': ln_gamma, 'ln_beta': ln_beta}
    _L0_gnn_all = _L0_gnn_setup()
    _L0_gnn_in = {k: v for k, v in _L0_gnn_all.items() if k in ('msg_W1', 'msg_b1', 'msg_W2', 'msg_b2', 'upd_W1', 'upd_b1', 'upd_W2', 'upd_b2', 'ln_gamma', 'ln_beta')}
    del _L0_gnn_all

    def _L1_gnn_setup():
        import jax, jax.numpy as jnp
        import numpy as np
        N_NODES = 50000
        N_EDGES = 9375
        D = 128
        N_GRAPHS = 64
        key = jax.random.key(seed)
        ks = jax.random.split(key, 10)
        inp = {'x': jax.random.normal(ks[0], (N_NODES, D), jnp.float32), 'edge_index': jax.random.randint(ks[1], (2, N_EDGES), 0, N_NODES, jnp.int64), 'edge_attr': jax.random.normal(ks[2], (N_EDGES, D), jnp.float32), 'u': jax.random.normal(ks[3], (N_GRAPHS, D), jnp.float32), 'batch': jnp.sort(jax.random.randint(ks[4], (N_NODES,), 0, N_GRAPHS, jnp.int64)), 'W1a': jax.random.normal(ks[5], (2 * D, 256), jnp.float32) * (1.0 / np.sqrt(2 * D)), 'b1a': jnp.zeros((256,), jnp.float32), 'W1b': jax.random.normal(ks[6], (256, D), jnp.float32) * (1.0 / 16.0), 'b1b': jnp.zeros((D,), jnp.float32), 'W2a': jax.random.normal(ks[7], (3 * D, 256), jnp.float32) * (1.0 / np.sqrt(3 * D)), 'b2a': jnp.zeros((256,), jnp.float32), 'W2b': jax.random.normal(ks[8], (256, D), jnp.float32) * (1.0 / 16.0), 'b2b': jnp.zeros((D,), jnp.float32)}
        return inp
    _L1_gnn_all = _L1_gnn_setup()
    _L1_gnn_in = {k: v for k, v in _L1_gnn_all.items() if k in ('u', 'W1a', 'b1a', 'W1b', 'b1b', 'W2a', 'b2a', 'W2b', 'b2b')}
    del _L1_gnn_all
    return {'x': x, 'src': src, 'dst': dst, 'edge_attr_128': edge_attr_128, 'L0_gnn_msg_W1': _L0_gnn_in['msg_W1'], 'L0_gnn_msg_b1': _L0_gnn_in['msg_b1'], 'L0_gnn_msg_W2': _L0_gnn_in['msg_W2'], 'L0_gnn_msg_b2': _L0_gnn_in['msg_b2'], 'L0_gnn_upd_W1': _L0_gnn_in['upd_W1'], 'L0_gnn_upd_b1': _L0_gnn_in['upd_b1'], 'L0_gnn_upd_W2': _L0_gnn_in['upd_W2'], 'L0_gnn_upd_b2': _L0_gnn_in['upd_b2'], 'L0_gnn_ln_gamma': _L0_gnn_in['ln_gamma'], 'L0_gnn_ln_beta': _L0_gnn_in['ln_beta'], 'L1_gnn_u': _L1_gnn_in['u'], 'L1_gnn_W1a': _L1_gnn_in['W1a'], 'L1_gnn_b1a': _L1_gnn_in['b1a'], 'L1_gnn_W1b': _L1_gnn_in['W1b'], 'L1_gnn_b1b': _L1_gnn_in['b1b'], 'L1_gnn_W2a': _L1_gnn_in['W2a'], 'L1_gnn_b2a': _L1_gnn_in['b2a'], 'L1_gnn_W2b': _L1_gnn_in['W2b'], 'L1_gnn_b2b': _L1_gnn_in['b2b']}

def reference(x, src, dst, edge_attr_128, L0_gnn_msg_W1, L0_gnn_msg_b1, L0_gnn_msg_W2, L0_gnn_msg_b2, L0_gnn_upd_W1, L0_gnn_upd_b1, L0_gnn_upd_W2, L0_gnn_upd_b2, L0_gnn_ln_gamma, L0_gnn_ln_beta, L1_gnn_u, L1_gnn_W1a, L1_gnn_b1a, L1_gnn_W1b, L1_gnn_b1b, L1_gnn_W2a, L1_gnn_b2a, L1_gnn_W2b, L1_gnn_b2b):
    import jax
    import jax.numpy as jnp

    def _L0_gnn_ref(x, edge_index, edge_attr, msg_W1, msg_b1, msg_W2, msg_b2, upd_W1, upd_b1, upd_W2, upd_b2, ln_gamma, ln_beta):
        import jax, jax.numpy as jnp
        import numpy as np
        N_NODES = 50000
        N_EDGES = 10000
        HID = 128
        LN_EPS = 1e-05

        def _layer_norm(h, gamma, beta):
            mu = jnp.mean(h, axis=-1, keepdims=True)
            var = jnp.mean(jnp.square(h - mu), axis=-1, keepdims=True)
            return (h - mu) * jax.lax.rsqrt(var + LN_EPS) * gamma + beta
        src, dst = (edge_index[0], edge_index[1])
        msg_in = jnp.concatenate([x[src], x[dst], edge_attr], axis=-1)
        h = jax.nn.relu(msg_in @ msg_W1 + msg_b1)
        messages = h @ msg_W2 + msg_b2
        aggregated = jax.ops.segment_sum(messages, dst, num_segments=x.shape[0])
        upd_in = jnp.concatenate([x, aggregated], axis=-1)
        u = jax.nn.relu(upd_in @ upd_W1 + upd_b1)
        updated = u @ upd_W2 + upd_b2
        return _layer_norm(x + updated, ln_gamma, ln_beta)

    def _L1_gnn_ref(x, edge_index, edge_attr, u, batch, W1a, b1a, W1b, b1b, W2a, b2a, W2b, b2b):
        import jax, jax.numpy as jnp
        import numpy as np
        N_NODES = 50000
        N_EDGES = 9375
        D = 128
        N_GRAPHS = 64
        row, col = (edge_index[0], edge_index[1])
        h = jnp.concatenate([x[row], edge_attr], axis=1)
        h = jax.nn.relu(h @ W1a + b1a) @ W1b + b1b
        s = jax.ops.segment_sum(h, col, num_segments=x.shape[0])
        cnt = jax.ops.segment_sum(jnp.ones((col.shape[0],), x.dtype), col, num_segments=x.shape[0])
        agg = s / jnp.maximum(cnt, 1.0)[:, None]
        h2 = jnp.concatenate([x, agg, u[batch]], axis=1)
        return jax.nn.relu(h2 @ W2a + b2a) @ W2b + b2b
    edge_index = jnp.stack([src, dst])
    batch0 = jnp.zeros((100000,), jnp.int32)
    h = jnp.maximum(_layernorm(x, axis=-1), 0.0)
    x = x + _L0_gnn_ref(h, edge_index, edge_attr_128, L0_gnn_msg_W1, L0_gnn_msg_b1, L0_gnn_msg_W2, L0_gnn_msg_b2, L0_gnn_upd_W1, L0_gnn_upd_b1, L0_gnn_upd_W2, L0_gnn_upd_b2, L0_gnn_ln_gamma, L0_gnn_ln_beta)
    h = jnp.maximum(_layernorm(x, axis=-1), 0.0)
    x = x + _L1_gnn_ref(h, edge_index, edge_attr_128, L1_gnn_u, batch0, L1_gnn_W1a, L1_gnn_b1a, L1_gnn_W1b, L1_gnn_b1b, L1_gnn_W2a, L1_gnn_b2a, L1_gnn_W2b, L1_gnn_b2b)
    return x

_drawn_inputs = setup_inputs


def setup_inputs(seed=0):
    import zlib

    import numpy as np

    out = dict(_drawn_inputs(seed))
    spreads = {'L0_gnn_msg_b1': (0.0, 0.725),
     'L0_gnn_msg_b2': (0.0, 0.508),
     'L0_gnn_upd_b1': (0.0, 0.1),
     'L0_gnn_upd_b2': (0.0, 0.1),
     'L0_gnn_ln_gamma': (1.0, 0.2),
     'L0_gnn_ln_beta': (0.0, 0.1),
     'L1_gnn_b1a': (0.0, 0.8),
     'L1_gnn_b1b': (0.0, 0.8),
     'L1_gnn_b2a': (0.0, 0.1),
     'L1_gnn_b2b': (0.0, 0.1)}
    factors = {}
    for name, (base, spread) in spreads.items():
        noise = np.random.default_rng([zlib.crc32(name.encode()), seed]).standard_normal(out[name].shape)
        drawn = base * np.exp(spread * noise) if base else spread * noise
        out[name] = jnp.asarray(drawn.astype(out[name].dtype))
    for name, factor in factors.items():
        out[name] = (out[name] * factor).astype(out[name].dtype)
    return out
```

```python
from contextlib import ExitStack

import concourse.bass as bass
from concourse import mybir

F32 = mybir.dt.float32
BF16 = mybir.dt.bfloat16
I32 = mybir.dt.int32
ALU = mybir.AluOpType
ACT = mybir.ActivationFunctionType

P = 128
TILES = 4
GROUP = TILES * P
UNROLL = 4
LN_EPS = 1e-5
NO_ROW = 1 << 20


class At:

    def __init__(self, turn, slot):
        self.turn, self.slot = turn, slot

    def __add__(self, lag):
        return At(self.turn + (self.slot + lag) // UNROLL, (self.slot + lag) % UNROLL)

    @property
    def index(self):
        return self.turn * UNROLL + self.slot

    @property
    def done(self):
        return self.turn * UNROLL + (self.slot + 1)

    @property
    def landed(self):
        return self.turn * 16 + 16

    def inside(self, groups):
        return not isinstance(self.turn, int) or 0 <= self.index < groups


def steps(eng, body, first, end, loop_turns):
    a, b = loop_turns
    for i in range(first, a * UNROLL):
        body(At(i // UNROLL, i % UNROLL))
    if b > a:
        with eng.Fori(a, b) as turn:
            for slot in range(UNROLL):
                body(At(turn, slot))
    for i in range(b * UNROLL, end):
        body(At(i // UNROLL, i % UNROLL))


def build(nc, x, edge_attr, src_cols, dst_cols, next_cols, dst_rows, prev_rows,
          msg_W1, msg_b1, msg_W2, msg_b2, upd_W1, upd_b1, upd_W2, upd_b2, ln_gamma, ln_beta,
          glob_u, W1a, b1a, W1b, b1b, W2a, b2a, W2b, b2b, out):
    n_nodes, D = x.shape
    NG = -(-n_nodes // GROUP)
    EG = src_cols.shape[0]
    n_edges = EG * GROUP
    assert D == P and NG > 12 and EG >= 8

    x1 = nc.dram_tensor("x1_scratch", [n_nodes, D], F32, kind="Internal").ap()
    x1_edge = nc.dram_tensor("x1_edge_scratch", [n_edges, D], F32, kind="Internal").ap()
    same_d = nc.dram_tensor("same_scratch", [EG, GROUP], F32, kind="Internal").ap()
    rcount_d = nc.dram_tensor("rcount_scratch", [EG, GROUP], F32, kind="Internal").ap()
    rowidx_d = nc.dram_tensor("rowidx_scratch", [EG, P, TILES], I32, kind="Internal").ap()
    carry_d = nc.dram_tensor("carry_scratch", [3, EG + 1], F32, kind="Internal").ap()

    ctx = ExitStack()
    with ctx:
        def sb(name, shape, dt=F32):
            return ctx.enter_context(nc.sbuf_tensor(name, shape, dt))

        def ring(name, n, shape, dt=F32):
            return [sb(f"{name}{k}", shape, dt) for k in range(n)]

        def sem(name):
            return ctx.enter_context(nc.semaphore(name))

        def sems(prefix, names):
            return {n: sem(f"{prefix}_{n}") for n in names.split()}

        def slot_sems(name):
            return [sem(f"{name}{k}") for k in range(UNROLL)]

        ident = sb("ident", [P, P])
        eps = sb("eps", [P, 1])
        gamma_b = sb("gamma_b", [P, P])
        beta_b = sb("beta_b", [P, P])
        b2b_b = sb("b2b_b", [P, P])
        msg_W1s = sb("msg_W1s", [P, 3, P])
        msg_W2s = sb("msg_W2s", [P, P])
        upd_W1s = sb("upd_W1s", [P, 2, P])
        upd_W2s = sb("upd_W2s", [P, P])
        W1as = sb("W1as", [P, 2, 2 * P])
        W1bs = sb("W1bs", [P, 2, P])
        W2as = sb("W2as", [P, 3, 2 * P])
        W2bs = sb("W2bs", [P, 2, P])
        cols = sb("cols", [P, 10])
        MSG_B1, MSG_B2, UPD_B1, B1A, B1B, B2A, GLOB = 0, 1, 2, 3, 5, 6, 8
        b2a_full = sb("b2a_full", [P, 2])
        ones3 = sb("ones3", [3, P], BF16)
        bias_f = sb("bias_f", [1, 2, P])
        bias_rest = sb("bias_rest", [1, 2, 2, P])
        bias_parts = sb("bias_parts", [1, 3, 2, GROUP], BF16)
        bias_rows = sb("bias_rows", [3, 2, GROUP], BF16)
        UPD_B2, B2B = 0, 1
        dstc = sb("dstc", [P, EG, TILES], I32)
        nextc = sb("nextc", [P, EG, TILES], I32)
        samec = sb("samec", [P, EG, TILES])
        rowidx = sb("rowidx", [P, EG, TILES], I32)
        dstr = sb("dstr", [EG, GROUP], I32)
        prevr = sb("prevr", [EG, GROUP], I32)
        samer = sb("samer", [EG, GROUP])
        ones_r = sb("ones_r", [EG, GROUP])
        zeros_r = sb("zeros_r", [EG, GROUP])
        count = sb("count", [EG, GROUP])
        through = sb("through", [EG, GROUP])
        count2 = sb("count2", [EG, GROUP])
        count3 = sb("count3", [EG, GROUP])
        rcount = sb("rcount", [EG, GROUP])
        ends = sb("ends", [1, 2, EG])
        carries = sb("carries", [1, EG + 1])
        carry_in = sb("carry_in", [EG, 1])

        big = [P, GROUP]
        A4 = ring("A4_", 4, big)
        B4 = ring("B4_", 4, big)
        C4 = ring("C4_", 4, big)
        D4 = ring("D4_", 4, big)
        E4 = ring("E4_", 4, big)
        F4 = ring("F4_", 4, big)
        G2 = ring("G2_", 2, big)
        t2 = ring("t_", 2, big)
        that2 = ring("that_", 2, big)
        scaled2 = ring("scaled_", 2, big)
        xb2 = ring("xb_", 2, big)
        aT = ring("aT_", 2, big)
        bT = ring("bT_", 2, big)
        cT = ring("cT_", 2, big)
        dT = ring("dT_", 2, [P, 2, GROUP])
        eT = ring("eT_", 2, [P, 2, GROUP])
        zT = ring("zT_", 2, big)
        sT = ring("sT_", 2, big)
        mT = ring("mT_", 2, big)
        same2 = ring("same_", 2, big)
        rc2 = ring("rc_", 2, big)
        srcidx = ring("srcidx_", 4, [P, TILES], I32)
        dstidx = ring("dstidx_", 4, [P, TILES], I32)
        outidx = ring("outidx_", 4, [P, TILES], I32)
        st = [ring(f"st{k}_", 2, [P, TILES, 6]) for k in range(3)]
        mean = [ring(f"mean{k}_", 4, [P, TILES]) for k in range(3)]
        sumsq = [ring(f"sumsq{k}_", 4, [P, TILES]) for k in range(3)]
        half = [ring(f"half{k}_", 2, [P, 3, TILES]) for k in range(3)]
        sd = [ring(f"sd{k}_", 4, [P, TILES]) for k in range(3)]
        rstd = [ring(f"rstd{k}_", 4, [P, TILES]) for k in range(3)]

        bank = [ctx.enter_context(nc.psum_tensor(f"bank{k}", big, F32)) for k in range(8)]

        weights_in = sem("weights_in")
        bias_cols_in = sem("bias_cols_in")
        edge_lists_in = sem("edge_lists_in")
        ident_ready = sem("ident_ready")
        const_ready = sem("const_ready")
        bias_chain = sem("bias_chain")
        bias_rows_in = sem("bias_rows_in")
        glob_ready = sem("glob_ready")
        b2a_ready = sem("b2a_ready")
        lists = sems("lists", "idx idx_out same count ends_out ends_in carry carry_out carry_in rcount rcount_out")
        N = sems("n", "x_link t_link x1_link x_var x_sd xn hT_ps hT u_ps uT d_ps t t_var t_sd that scaled xb x1 "
                      "x1_var x1_sd x1n h1T_ps h1T v0_ps v1_ps v0T v1T o_ps out")
        n_x_in = slot_sems("n_x_in")
        n_x1_stored = slot_sems("n_x1_stored")
        n_out_stored = slot_sems("n_out_stored")
        edge_sems = ("xs_link xd_link t_link x_var x_sd xsn xdn sT_ps dT_ps aT_ps sT dT aT m_ps mT z_ps zT sum "
                     "agg u_ps uT d_ps xb t t_var t_sd that scaled new")
        E = sems("e", edge_sems)
        e_idx_in = [slot_sems(f"e{k}_idx_in") for k in (0, 1)]
        e_src_in = [slot_sems(f"e{k}_src_in") for k in (0, 1)]
        e_dst_in = [slot_sems(f"e{k}_dst_in") for k in (0, 1)]
        e_attr_in = [slot_sems(f"e{k}_attr_in") for k in (0, 1)]
        e_same_in = [slot_sems(f"e{k}_same_in") for k in (0, 1)]
        e_outidx_in = [slot_sems(f"e{k}_outidx_in") for k in (0, 1)]
        e_new_stored = slot_sems("e0_new_stored")
        e_scattered = [slot_sems(f"e{k}_scattered") for k in (0, 1)]

        N_WEIGHT_DMAS = 11
        N_COL_DMAS = 11

        N_STEPS = (-2, NG + 5)
        N_LOOP = (2, (NG - 3) // UNROLL)
        E_STEPS = (-4, EG + 3)
        E_LOOP = (1, (EG - 4) // UNROLL)

        def wait_all(eng, pairs):
            for _, count_ in pairs:
                if not isinstance(count_, int):
                    eng.lower_val(count_)
            eng.wait_ge(ident_ready, 2)
            for semaphore, count_ in pairs:
                eng.wait_ge(semaphore, count_)

        def done_by(layer):
            return lambda g: g.done + layer * EG

        def node_rows(t, g):
            if isinstance(g.turn, int) and g.index == NG - 1:
                rows = t[n_nodes - GROUP:n_nodes, :]
            else:
                rows = t[bass.ds(g.index * GROUP, GROUP), :]
            return rows.rearrange("(p j) f -> p (j f)", p=P)

        def edge_rows(t, g):
            return t[bass.ds(g.index * GROUP, GROUP), :].rearrange("(j p) f -> p j f", p=P)

        def tiles(t):
            return t[:, :].rearrange("p (j f) -> p j f", j=TILES)

        def list_row(t, g):
            row = t[bass.ds(g.index, 1), :]
            return row.broadcast_to([P, GROUP])

        def all_stored(eng, slots, groups, each=1):
            for k in range(UNROLL):
                eng.wait_ge(slots[k], 16 * each * len(range(k, groups, UNROLL)))

        def nodes_are_done(eng):
            eng.wait_ge(N["out"], NG)
            all_stored(eng, n_x1_stored, NG)
            all_stored(eng, n_out_stored, NG)

        def edges0_are_done(eng):
            eng.wait_ge(E["new"], EG)
            all_stored(eng, e_new_stored, EG)
            all_stored(eng, e_scattered[0], EG, TILES)

        block = ctx.enter_context(nc.Block())

        @block.sync
        def _(sp):
            for col, src, k in ((MSG_B1, msg_b1, 1), (MSG_B2, msg_b2, 1), (UPD_B1, upd_b1, 1), (B1A, b1a, 2),
                                (B1B, b1b, 1), (B2A, b2a, 2), (GLOB, glob_u[0, :], 1)):
                for h in range(k):
                    sp.dma_start(cols[:, col + h:col + h + 1],
                                 src[h * P:(h + 1) * P].rearrange("(p o) -> p o", o=1)).then_inc(bias_cols_in, 16)
            sp.dma_start(bias_f[:, UPD_B2, :], upd_b2.rearrange("(o f) -> o f", o=1)).then_inc(bias_cols_in, 16)
            sp.dma_start(bias_f[:, B2B, :], b2b.rearrange("(o f) -> o f", o=1)).then_inc(bias_cols_in, 16)
            for dst, src in ((gamma_b, ln_gamma), (beta_b, ln_beta), (b2b_b, b2b)):
                sp.dma_start(dst[:, :], src.rearrange("(o f) -> o f", o=1).broadcast_to([P, P])).then_inc(weights_in, 16)
            for dst, src in ((msg_W1s, msg_W1), (upd_W1s, upd_W1), (W1as, W1a), (W1bs, W1b), (W2as, W2a), (W2bs, W2b)):
                sp.dma_start(dst[:, :, :], src.rearrange("(k p) n -> p k n", p=P)).then_inc(weights_in, 16)
            sp.dma_start(msg_W2s[:, :], msg_W2).then_inc(weights_in, 16)
            sp.dma_start(upd_W2s[:, :], upd_W2).then_inc(weights_in, 16)
            sp.dma_start(dstc[:, :, :], dst_cols.rearrange("g p j -> p g j")).then_inc(edge_lists_in, 16)
            sp.dma_start(nextc[:, :, :], next_cols.rearrange("g p j -> p g j")).then_inc(edge_lists_in, 16)
            sp.dma_start(dstr[:, :], dst_rows).then_inc(edge_lists_in, 16)
            sp.dma_start(prevr[:, :], prev_rows).then_inc(edge_lists_in, 16)
            sp.wait_ge(bias_chain, 8)
            for k in range(3):
                sp.dma_start(bias_rows[k:k + 1, :, :], bias_parts[:, k, :, :]).then_inc(bias_rows_in, 16)
            sp.wait_ge(lists["idx"], 2)
            sp.dma_start(rowidx_d.rearrange("g p j -> p g j"), rowidx[:, :, :]).then_inc(lists["idx_out"], 16)
            sp.wait_ge(lists["same"], 1)
            sp.dma_start(same_d, samer[:, :]).then_inc(lists["idx_out"], 16)
            sp.wait_ge(lists["count"], 2)
            sp.dma_start(carry_d[0:1, 0:EG].rearrange("o g -> g o"), count[:, GROUP - 1:GROUP]).then_inc(lists["ends_out"], 16)
            sp.dma_start(carry_d[1:2, 0:EG].rearrange("o g -> g o"), through[:, GROUP - 1:GROUP]).then_inc(lists["ends_out"], 16)
            sp.wait_ge(lists["ends_out"], 32)
            sp.dma_start(ends[:, 0, :], carry_d[0:1, 0:EG]).then_inc(lists["ends_in"], 16)
            sp.dma_start(ends[:, 1, :], carry_d[1:2, 0:EG]).then_inc(lists["ends_in"], 16)
            sp.wait_ge(lists["carry"], 2)
            sp.dma_start(carry_d[2:3, :], carries[:, :]).then_inc(lists["carry_out"], 16)
            sp.wait_ge(lists["carry_out"], 16)
            sp.dma_start(carry_in[:, :], carry_d[2:3, 0:EG].rearrange("o g -> g o")).then_inc(lists["carry_in"], 16)
            sp.wait_ge(lists["rcount"], 3)
            sp.dma_start(rcount_d, rcount[:, :]).then_inc(lists["rcount_out"], 16)

            def node_step(i):
                g = i + 2
                if g.inside(NG):
                    if (g + -4).inside(NG):
                        sp.wait_ge(N["x1"], (g + -4).done)
                    sp.dma_start(A4[g.slot][:, :], node_rows(x, g)).then_inc(n_x_in[g.slot], 16)
                g = i + -2
                if g.inside(NG):
                    sp.wait_ge(N["x1"], g.done)
                    if isinstance(g.turn, int) and g.index == NG - 1:
                        p = g + -1
                        sp.wait_ge(n_x1_stored[p.slot], p.landed)
                    sp.dma_start(node_rows(x1, g), C4[g.slot][:, :]).then_inc(n_x1_stored[g.slot], 16)
                g = i + -5
                if g.inside(NG):
                    sp.wait_ge(N["out"], g.done)
                    if isinstance(g.turn, int) and g.index == NG - 1:
                        p = g + -1
                        sp.wait_ge(n_out_stored[p.slot], p.landed)
                    sp.dma_start(node_rows(out, g), D4[g.slot][:, :]).then_inc(n_out_stored[g.slot], 16)

            steps(sp, node_step, *N_STEPS, N_LOOP)

            def edge_step(i, layer):
                S, n = E, done_by(layer)
                g = i + 4
                if g.inside(EG):
                    if (g + -4).inside(EG):
                        sp.wait_ge(e_src_in[layer][g.slot], (g + -4).landed * TILES)
                        if layer == 0:
                            sp.wait_ge(e_dst_in[layer][g.slot], (g + -4).landed * TILES)
                    sp.dma_start(srcidx[g.slot][:, :], src_cols[bass.ds(g.index, 1), :, :].rearrange("o p j -> (o p) j")
                                 ).then_inc(e_idx_in[layer][g.slot], 16)
                    if layer == 0:
                        sp.dma_start(dstidx[g.slot][:, :], dst_cols[bass.ds(g.index, 1), :, :].rearrange("o p j -> (o p) j")
                                     ).then_inc(e_idx_in[layer][g.slot], 16)
                g = i + 3
                if layer == 1 and g.inside(EG):
                    if (g + -4).inside(EG):
                        sp.wait_ge(S["xb"], n(g + -4))
                        sp.wait_ge(S["xdn"], n(g + -4))
                    sp.dma_start(tiles(B4[g.slot]), edge_rows(x1_edge, g)).then_inc(e_dst_in[1][g.slot], 16)
                g = i + 2
                if g.inside(EG):
                    if (g + -4).inside(EG):
                        sp.wait_ge(S["aT_ps"], n(g + -4))
                    sp.dma_start(tiles(D4[g.slot]), edge_rows(edge_attr, g)).then_inc(e_attr_in[layer][g.slot], 16)
                g = i
                if g.inside(EG):
                    if (g + -2).inside(EG):
                        wait_all(sp, [(S["agg"], n(g + -2))])
                    sp.dma_start(same2[g.slot % 2][:, :], list_row(same_d, g)).then_inc(e_same_in[layer][g.slot], 16)
                    if layer == 1:
                        sp.dma_start(rc2[g.slot % 2][:, :], list_row(rcount_d, g)).then_inc(e_same_in[layer][g.slot], 16)
                    if (g + -4).inside(EG):
                        sp.wait_ge(e_scattered[layer][g.slot], (g + -4).landed * TILES)
                    sp.dma_start(outidx[g.slot][:, :], rowidx_d[bass.ds(g.index, 1), :, :].rearrange("o p j -> (o p) j")
                                 ).then_inc(e_outidx_in[layer][g.slot], 16)
                g = i + -3
                if layer == 0 and g.inside(EG):
                    sp.wait_ge(S["new"], n(g))
                    sp.dma_start(edge_rows(x1_edge, g), tiles(F4[g.slot])).then_inc(e_new_stored[g.slot], 16)

            sp.wait_ge(lists["idx_out"], 32)
            sp.wait_ge(lists["rcount_out"], 16)
            nodes_are_done(sp)
            steps(sp, lambda i: edge_step(i, 0), *E_STEPS, E_LOOP)
            edges0_are_done(sp)
            steps(sp, lambda i: edge_step(i, 1), *E_STEPS, E_LOOP)
            all_stored(sp, e_scattered[1], EG, TILES)

        @block.tensor
        def _(pe):
            def transpose4(ps, src):
                for j in range(TILES):
                    last = pe.transpose(ps[:, j * P:(j + 1) * P], src[:, j * P:(j + 1) * P], ident[:, :])
                return last

            pe.wait_ge(weights_in, 16 * N_WEIGHT_DMAS)
            pe.wait_ge(bias_cols_in, 16 * N_COL_DMAS)
            pe.wait_ge(ident_ready, 2)
            for h in range(2):
                last = pe.matmul(bank[0][:, h:h + 1], W2as[:, 2, h * P:(h + 1) * P], cols[:, GLOB:GLOB + 1],
                                 start=True, stop=True)
            last.then_inc(glob_ready, 1)
            pe.wait_ge(b2a_ready, 1)
            pe.wait_ge(const_ready, 1)
            pe.wait_ge(bias_rows_in, 48)

            def node_step(i):
                hT_ps, h1T_ps, u_ps, d_ps, v0_ps, v1_ps, o_ps = bank[0:7]
                g = i + -3
                if g.inside(NG):
                    s = g.slot % 2
                    pe.wait_ge(N["h1T"], g.done)
                    for h, ps in ((0, v0_ps), (1, v1_ps)):
                        pe.matmul(ps[:, :], W2as[:, 0, h * P:(h + 1) * P], bT[s][:, :],
                                  start=True, stop=True).then_inc(N["v0_ps" if h == 0 else "v1_ps"], 1)
                g = i
                if g.inside(NG):
                    pe.wait_ge(N["hT"], g.done)
                    pe.matmul(u_ps[:, :], upd_W1s[:, 0, :], aT[g.slot % 2][:, :], start=True, stop=True
                              ).then_inc(N["u_ps"], 1)
                g = i + -2
                if g.inside(NG):
                    pe.wait_ge(N["x1n"], g.done)
                    transpose4(h1T_ps, G2[g.slot % 2]).then_inc(N["h1T_ps"], 1)
                g = i + -3
                if g.inside(NG):
                    s = g.slot % 2
                    if (g + -1).inside(NG):
                        pe.wait_ge(N["out"], (g + -1).done)
                    pe.matmul(o_ps[:, :], ones3[:, :], bias_rows[:, B2B, :], start=True, stop=False)
                    pe.wait_ge(N["v0T"], g.done)
                    pe.wait_ge(N["v1T"], g.done)
                    for j in range(TILES):
                        for h in range(2):
                            last = pe.matmul(o_ps[:, j * P:(j + 1) * P], dT[s][:, h, j * P:(j + 1) * P], W2bs[:, h, :],
                                             start=False, stop=(j == TILES - 1 and h == 1))
                    last.then_inc(N["o_ps"], 1)
                g = i + 1
                if g.inside(NG):
                    pe.wait_ge(N["xn"], g.done)
                    transpose4(hT_ps, B4[g.slot]).then_inc(N["hT_ps"], 1)
                g = i
                if g.inside(NG):
                    if (g + -1).inside(NG):
                        pe.wait_ge(N["t"], (g + -1).done)
                    pe.matmul(d_ps[:, :], ones3[:, :], bias_rows[:, UPD_B2, :], start=True, stop=False)
                    pe.wait_ge(N["uT"], g.done)
                    for j in range(TILES):
                        last = pe.matmul(d_ps[:, j * P:(j + 1) * P], cT[g.slot % 2][:, j * P:(j + 1) * P], upd_W2s[:, :],
                                         start=False, stop=(j == TILES - 1))
                    last.then_inc(N["d_ps"], 1)

            steps(pe, node_step, *N_STEPS, N_LOOP)

            def edge_step(i, layer):
                S, n = E, done_by(layer)
                halves = 1 + layer
                msg_in = msg_W1s if layer == 0 else W1as
                msg_out = msg_W2s[:, :].rearrange("p (h n) -> p h n", h=1) if layer == 0 else W1bs
                upd_in = upd_W1s if layer == 0 else W2as
                upd_out = upd_W2s[:, :].rearrange("p (h n) -> p h n", h=1) if layer == 0 else W2bs
                ta_ps, tb_ps, z_ps, d_ps = bank[0:4]
                m_ps, u_ps = bank[4:6], bank[6:8]
                g = i
                if g.inside(EG):
                    s = g.slot % 2
                    pe.wait_ge(S["sT"], n(g))
                    pe.wait_ge(S["dT"], n(g))
                    pe.wait_ge(S["aT"], n(g))
                    parts = [aT[s], bT[s], cT[s]] if layer == 0 else [aT[s], cT[s]]
                    for h in range(halves):
                        for k, part in enumerate(parts):
                            last = pe.matmul(m_ps[h][:, :], msg_in[:, k, h * P:(h + 1) * P], part[:, :],
                                             start=(k == 0), stop=(k == len(parts) - 1))
                    last.then_inc(S["m_ps"], 1)
                g = i + -1
                if g.inside(EG):
                    s = g.slot % 2
                    pe.wait_ge(S["agg"], n(g))
                    agg = sT[s] if layer == 0 else mT[s]
                    for h in range(halves):
                        pe.matmul(u_ps[h][:, :], upd_in[:, 0, h * P:(h + 1) * P], bT[s][:, :], start=True, stop=False)
                        last = pe.matmul(u_ps[h][:, :], upd_in[:, 1, h * P:(h + 1) * P], agg[:, :], start=False, stop=True)
                    last.then_inc(S["u_ps"], 1)
                g = i
                if g.inside(EG):
                    s = g.slot % 2
                    pe.wait_ge(S["mT"], n(g))
                    for h in range(halves):
                        last = pe.matmul(z_ps[:, :], msg_out[:, h, :], dT[s][:, h, :], start=(h == 0), stop=(h == halves - 1))
                    last.then_inc(S["z_ps"], 1)
                g = i + 1
                if g.inside(EG):
                    s = g.slot % 2
                    pe.wait_ge(S["xsn"], n(g))
                    transpose4(ta_ps, G2[s]).then_inc(S["sT_ps"], 1)
                    pe.wait_ge(S["xdn"], n(g))
                    transpose4(tb_ps, C4[g.slot]).then_inc(S["dT_ps"], 1)
                    pe.wait_ge(e_attr_in[layer][g.slot], g.landed)
                    pe.wait_ge(S["sT"], n(g))
                    transpose4(ta_ps, D4[g.slot]).then_inc(S["aT_ps"], 1)
                g = i + -1
                if g.inside(EG):
                    s = g.slot % 2
                    if (g + -1).inside(EG):
                        pe.wait_ge(S["t" if layer == 0 else "new"], n(g + -1))
                    if layer == 0:
                        pe.matmul(d_ps[:, :], ones3[:, :], bias_rows[:, UPD_B2, :], start=True, stop=False)
                    pe.wait_ge(S["uT"], n(g))
                    for j in range(TILES):
                        for h in range(halves):
                            last = pe.matmul(d_ps[:, j * P:(j + 1) * P], eT[s][:, h, j * P:(j + 1) * P], upd_out[:, h, :],
                                             start=(layer == 1 and h == 0),
                                             stop=(h == halves - 1 and (layer == 1 or j == TILES - 1)))
                    last.then_inc(S["d_ps"], 1)

            nodes_are_done(pe)
            steps(pe, lambda i: edge_step(i, 0), *E_STEPS, E_LOOP)
            edges0_are_done(pe)
            steps(pe, lambda i: edge_step(i, 1), *E_STEPS, E_LOOP)

        @block.scalar
        def _(act):
            def relu(out_, in_, bias=None):
                if bias is None:
                    return act.activation(out_, in_, ACT.Relu)
                return act.activation(out_, in_, ACT.Relu, bias=bias)

            def root(k, g):
                return act.activation(sd[k][g.slot][:, :], sumsq[k][g.slot][:, :], ACT.Sqrt, bias=eps[:, :], scale=1.0 / D)

            act.wait_ge(const_ready, 1)
            act.wait_ge(bias_cols_in, 16 * N_COL_DMAS)
            act.wait_ge(b2a_ready, 1)

            def node_step(i):
                hT_ps, h1T_ps, u_ps, d_ps, v0_ps, v1_ps, o_ps = bank[0:7]
                g = i + -3
                if g.inside(NG):
                    act.wait_ge(N["v0_ps"], g.done)
                    relu(dT[g.slot % 2][:, 0, :], v0_ps[:, :], b2a_full[:, 0:1]).then_inc(N["v0T"], 1)
                g = i + -1
                if g.inside(NG):
                    act.wait_ge(N["t_var"], g.done)
                    root(1, g).then_inc(N["t_sd"], 1)
                g = i + -3
                if g.inside(NG):
                    act.wait_ge(N["v1_ps"], g.done)
                    relu(dT[g.slot % 2][:, 1, :], v1_ps[:, :], b2a_full[:, 1:2]).then_inc(N["v1T"], 1)
                g = i + 1
                if g.inside(NG):
                    act.wait_ge(N["x_var"], g.done)
                    root(0, g).then_inc(N["x_sd"], 1)
                g = i
                if g.inside(NG):
                    act.wait_ge(N["u_ps"], g.done)
                    relu(cT[g.slot % 2][:, :], u_ps[:, :], cols[:, UPD_B1:UPD_B1 + 1]).then_inc(N["uT"], 1)
                g = i + -2
                if g.inside(NG):
                    act.wait_ge(N["h1T_ps"], g.done)
                    relu(bT[g.slot % 2][:, :], h1T_ps[:, :]).then_inc(N["h1T"], 1)
                g = i + 1
                if g.inside(NG):
                    act.wait_ge(N["hT_ps"], g.done)
                    relu(aT[g.slot % 2][:, :], hT_ps[:, :]).then_inc(N["hT"], 1)
                g = i + -1
                if g.inside(NG):
                    act.wait_ge(N["x1_var"], g.done)
                    root(2, g).then_inc(N["x1_sd"], 1)

            steps(act, node_step, *N_STEPS, N_LOOP)

            def edge_step(i, layer):
                S, n = E, done_by(layer)
                ta_ps, tb_ps, z_ps, d_ps = bank[0:4]
                m_ps, u_ps = bank[4:6], bank[6:8]
                g = i
                if g.inside(EG):
                    s = g.slot % 2
                    act.wait_ge(S["m_ps"], n(g))
                    for h in range(1 + layer):
                        col = MSG_B1 if layer == 0 else B1A + h
                        last = relu(dT[s][:, h, :], m_ps[h][:, :], cols[:, col:col + 1])
                    last.then_inc(S["mT"], 1)
                g = i + -1
                if g.inside(EG):
                    s = g.slot % 2
                    act.wait_ge(S["u_ps"], n(g))
                    for h in range(1 + layer):
                        bias = cols[:, UPD_B1:UPD_B1 + 1] if layer == 0 else b2a_full[:, h:h + 1]
                        last = relu(eT[s][:, h, :], u_ps[h][:, :], bias)
                    last.then_inc(S["uT"], 1)
                g = i
                if g.inside(EG):
                    s = g.slot % 2
                    act.wait_ge(S["z_ps"], n(g))
                    if (g + -2).inside(EG):
                        act.wait_ge(S["agg"], n(g + -2))
                    col = MSG_B2 if layer == 0 else B1B
                    act.activation(zT[s][:, :], z_ps[:, :], ACT.Identity, bias=cols[:, col:col + 1]).then_inc(S["zT"], 1)
                g = i + 2
                if g.inside(EG):
                    act.wait_ge(S["x_var"], n(g))
                    root(0, g)
                    root(1, g).then_inc(S["x_sd"], 1)
                g = i + 1
                if g.inside(EG):
                    s = g.slot % 2
                    act.wait_ge(S["sT_ps"], n(g))
                    relu(aT[s][:, :], ta_ps[:, :]).then_inc(S["sT"], 1)
                    act.wait_ge(S["dT_ps"], n(g))
                    relu(bT[s][:, :], tb_ps[:, :]).then_inc(S["dT"], 1)
                    act.wait_ge(S["aT_ps"], n(g))
                    act.activation(cT[s][:, :], ta_ps[:, :], ACT.Copy).then_inc(S["aT"], 1)
                g = i + -2
                if layer == 0 and g.inside(EG):
                    act.wait_ge(S["t_var"], n(g))
                    root(2, g).then_inc(S["t_sd"], 1)

            nodes_are_done(act)
            steps(act, lambda i: edge_step(i, 0), *E_STEPS, E_LOOP)
            edges0_are_done(act)
            steps(act, lambda i: edge_step(i, 1), *E_STEPS, E_LOOP)

        @block.vector
        def _(dve):
            def stats(k, g, src, link, n):
                s = st[k][g.slot % 2]
                for j in range(TILES):
                    last = dve.bn_stats(s[:, j, :], src[:, j * P:(j + 1) * P])
                last.then_inc(link, 1)
                dve.wait_ge(link, 4 * n - 3)
                diff, sq, both = (half[k][g.slot % 2][:, r, :] for r in range(3))
                dve.tensor_tensor(both, s[:, :, 2], s[:, :, 5], ALU.add)
                dve.tensor_tensor(diff, s[:, :, 1], s[:, :, 4], ALU.subtract).then_inc(link, 1)
                dve.wait_ge(link, 4 * n - 2)
                dve.scalar_tensor_tensor(out=mean[k][g.slot][:, :], in0=diff, scalar=-0.5, in1=s[:, :, 1],
                                         op0=ALU.mult, op1=ALU.add)
                dve.scalar_tensor_tensor(out=sq, in0=diff, scalar=D / 4.0, in1=diff,
                                         op0=ALU.mult, op1=ALU.mult).then_inc(link, 1)
                dve.wait_ge(link, 4 * n - 1)
                return dve.tensor_tensor(sumsq[k][g.slot][:, :], sq, both, ALU.add)

            def invert(k, g, link, n):
                dve.reciprocal(rstd[k][g.slot][:, :], sd[k][g.slot][:, :]).then_inc(link, 1)
                dve.wait_ge(link, 4 * n)

            def norm(k, g, dst, src):
                for j in range(TILES):
                    last = dve.tensor_scalar(dst[:, j * P:(j + 1) * P], src[:, j * P:(j + 1) * P],
                                             mean[k][g.slot][:, j:j + 1], rstd[k][g.slot][:, j:j + 1],
                                             ALU.subtract, ALU.mult)
                return last

            dve.memset(eps[:, :], LN_EPS)
            dve.memset(ones3[:, :], 1.0)
            dve.memset(ones_r[:, :], 1.0)
            dve.memset(carries[:, :], 0.0)
            dve.memset(zeros_r[:, :], 0.0).then_inc(const_ready, 1)
            dve.wait_ge(const_ready, 1)
            dve.wait_ge(bias_cols_in, 16 * N_COL_DMAS)
            def wide(k):
                return bias_parts[:, k, :, :].rearrange("o b (j f) -> o b j f", j=TILES)
            rests = [bias_f[:, :, :], bias_rest[:, 0, :, :], bias_rest[:, 1, :, :]]
            n = 0
            for k in range(3):
                for b in range(2):
                    dve.tensor_copy(wide(k)[:, b, :, :],
                                    rests[k][:, b, :].unsqueeze(1).broadcast_to([1, TILES, P])).then_inc(bias_chain, 1)
                n += 2
                dve.wait_ge(bias_chain, n)
                if k < 2:
                    dve.tensor_tensor(rests[k + 1], rests[k], wide(k)[:, :, 0, :], ALU.subtract).then_inc(bias_chain, 1)
                    n += 1
                    dve.wait_ge(bias_chain, n)
            dve.wait_ge(glob_ready, 1)
            dve.tensor_tensor(b2a_full[:, :], bank[0][:, 0:2], cols[:, B2A:B2A + 2], ALU.add).then_inc(b2a_ready, 1)
            dve.wait_ge(edge_lists_in, 64)
            dve.tensor_tensor(samec[:, :, :], dstc[:, :, :], nextc[:, :, :], ALU.is_equal).then_inc(lists["idx"], 1)
            dve.wait_ge(lists["idx"], 1)
            dve.scalar_tensor_tensor(out=rowidx[:, :, :], in0=samec[:, :, :], scalar=float(NO_ROW), in1=dstc[:, :, :],
                                     op0=ALU.mult, op1=ALU.add).then_inc(lists["idx"], 1)
            dve.tensor_tensor(samer[:, :], dstr[:, :], prevr[:, :], ALU.is_equal).then_inc(lists["same"], 1)
            dve.wait_ge(lists["same"], 1)
            dve.tensor_tensor_scan(count[:, :], samer[:, :], ones_r[:, :], 0.0, ALU.mult, ALU.add).then_inc(lists["count"], 1)
            dve.tensor_tensor_scan(through[:, :], samer[:, :], zeros_r[:, :], 1.0, ALU.mult, ALU.add).then_inc(lists["count"], 1)
            dve.wait_ge(lists["ends_in"], 32)
            dve.tensor_tensor_scan(carries[:, 1:EG + 1], ends[:, 1, :], ends[:, 0, :], 0.0, ALU.mult, ALU.add
                                   ).then_inc(lists["carry"], 2)
            dve.wait_ge(lists["carry_in"], 16)
            dve.scalar_tensor_tensor(out=count2[:, :], in0=through[:, :], scalar=carry_in[:, 0:1], in1=count[:, :],
                                     op0=ALU.mult, op1=ALU.add).then_inc(lists["rcount"], 1)
            dve.wait_ge(lists["rcount"], 1)
            dve.tensor_scalar(count3[:, :], count2[:, :], 1.0, None, ALU.max).then_inc(lists["rcount"], 1)
            dve.wait_ge(lists["rcount"], 2)
            dve.reciprocal(rcount[:, :], count3[:, :]).then_inc(lists["rcount"], 1)

            def node_step(i):
                hT_ps, h1T_ps, u_ps, d_ps, v0_ps, v1_ps, o_ps = bank[0:7]
                g = i + -2
                if g.inside(NG):
                    dve.wait_ge(N["x1_sd"], g.done)
                    invert(2, g, N["x1_link"], g.done)
                    norm(2, g, G2[g.slot % 2], C4[g.slot]).then_inc(N["x1n"], 1)
                g = i + -4
                if g.inside(NG):
                    dve.wait_ge(N["o_ps"], g.done)
                    if (g + -4).inside(NG):
                        dve.wait_ge(n_out_stored[g.slot], (g + -4).landed)
                    dve.tensor_tensor(D4[g.slot][:, :], o_ps[:, :], C4[g.slot][:, :], ALU.add).then_inc(N["out"], 1)
                g = i + -1
                if g.inside(NG):
                    s = g.slot % 2
                    dve.wait_ge(N["d_ps"], g.done)
                    dve.scalar_tensor_tensor(out=t2[s][:, :], in0=B4[g.slot][:, :], scalar=0.0, in1=d_ps[:, :],
                                             op0=ALU.max, op1=ALU.add).then_inc(N["t"], 1)
                    dve.wait_ge(N["t"], g.done)
                    stats(1, g, t2[s], N["t_link"], g.done).then_inc(N["t_var"], 1)
                g = i + 1
                if g.inside(NG):
                    dve.wait_ge(n_x_in[g.slot], g.landed)
                    stats(0, g, A4[g.slot], N["x_link"], g.done).then_inc(N["x_var"], 1)
                g = i + -1
                if g.inside(NG):
                    s = g.slot % 2
                    dve.wait_ge(N["t_sd"], g.done)
                    invert(1, g, N["t_link"], g.done)
                    norm(1, g, that2[s], t2[s]).then_inc(N["that"], 1)
                g = i + 1
                if g.inside(NG):
                    dve.wait_ge(N["x_sd"], g.done)
                    invert(0, g, N["x_link"], g.done)
                    norm(0, g, B4[g.slot], A4[g.slot]).then_inc(N["xn"], 1)
                g = i + -1
                if g.inside(NG):
                    s = g.slot % 2
                    dve.wait_ge(N["scaled"], g.done)
                    dve.wait_ge(N["xb"], g.done)
                    if (g + -4).inside(NG):
                        dve.wait_ge(n_x1_stored[g.slot], (g + -4).landed)
                    dve.tensor_tensor(C4[g.slot][:, :], scaled2[s][:, :], xb2[s][:, :], ALU.add).then_inc(N["x1"], 1)
                    dve.wait_ge(N["x1"], g.done)
                    stats(2, g, C4[g.slot], N["x1_link"], g.done).then_inc(N["x1_var"], 1)

            steps(dve, node_step, *N_STEPS, N_LOOP)

            def edge_step(i, layer):
                S, n = E, done_by(layer)
                d_ps = bank[3]
                g = i + -1
                if g.inside(EG):
                    s = g.slot % 2
                    dve.wait_ge(e_same_in[layer][g.slot], g.landed * (1 + layer))
                    dve.wait_ge(S["zT"], n(g))
                    if (g + -1).inside(EG):
                        dve.wait_ge(S["agg"], n(g + -1))
                        before = sT[1 - s][:, GROUP - 1:GROUP]
                    else:
                        before = 0.0
                    dve.tensor_tensor_scan(sT[s][:, :], same2[s][:, :], zT[s][:, :], before, ALU.mult, ALU.add
                                           ).then_inc(S["agg" if layer == 0 else "sum"], 1)
                    if layer == 1:
                        dve.wait_ge(S["sum"], g.done)
                        dve.tensor_tensor(mT[s][:, :], sT[s][:, :], rc2[s][:, :], ALU.mult).then_inc(S["agg"], 1)
                g = i + 1
                if g.inside(EG):
                    dve.wait_ge(S["x_sd"], n(g))
                    invert(0, g, S["xs_link"], n(g))
                    invert(1, g, S["xd_link"], n(g))
                    norm(0, g, G2[g.slot % 2], A4[g.slot]).then_inc(S["xsn"], 1)
                    norm(1, g, C4[g.slot], B4[g.slot]).then_inc(S["xdn"], 1)
                g = i + -2
                if g.inside(EG):
                    s = g.slot % 2
                    dve.wait_ge(S["d_ps"], n(g))
                    if layer == 0:
                        dve.scalar_tensor_tensor(out=t2[s][:, :], in0=C4[g.slot][:, :], scalar=0.0, in1=d_ps[:, :],
                                                 op0=ALU.max, op1=ALU.add).then_inc(S["t"], 1)
                        dve.wait_ge(S["t"], n(g))
                        stats(2, g, t2[s], S["t_link"], n(g)).then_inc(S["t_var"], 1)
                    else:
                        dve.wait_ge(S["xb"], n(g))
                        if (g + -4).inside(EG):
                            dve.wait_ge(e_scattered[1][g.slot], (g + -4).landed * TILES)
                        dve.tensor_tensor(F4[g.slot][:, :], d_ps[:, :], E4[g.slot][:, :], ALU.add).then_inc(S["new"], 1)
                g = i + 2
                if g.inside(EG):
                    dve.wait_ge(e_src_in[layer][g.slot], g.landed * TILES)
                    stats(0, g, A4[g.slot], S["xs_link"], n(g))
                    dve.wait_ge(e_dst_in[layer][g.slot], g.landed * (TILES if layer == 0 else 1))
                    stats(1, g, B4[g.slot], S["xd_link"], n(g)).then_inc(S["x_var"], 1)
                g = i + -2
                if layer == 0 and g.inside(EG):
                    s = g.slot % 2
                    dve.wait_ge(S["t_sd"], n(g))
                    invert(2, g, S["t_link"], n(g))
                    norm(2, g, that2[s], t2[s]).then_inc(S["that"], 1)
                    dve.wait_ge(S["scaled"], n(g))
                    dve.wait_ge(S["xb"], n(g))
                    if (g + -4).inside(EG):
                        dve.wait_ge(e_scattered[0][g.slot], (g + -4).landed * TILES)
                        dve.wait_ge(e_new_stored[g.slot], (g + -4).landed)
                    dve.tensor_tensor(F4[g.slot][:, :], scaled2[s][:, :], E4[g.slot][:, :], ALU.add).then_inc(S["new"], 1)

            nodes_are_done(dve)
            steps(dve, lambda i: edge_step(i, 0), *E_STEPS, E_LOOP)
            edges0_are_done(dve)
            steps(dve, lambda i: edge_step(i, 1), *E_STEPS, E_LOOP)

        @block.gpsimd
        def _(pool):
            pool.memset(ident[:, :], 0.0).then_inc(ident_ready, 1)
            pool.wait_ge(ident_ready, 1)
            pool.affine_select(out=ident[:, :], in_=ident[:, :], compare_op=ALU.not_equal, fill=1.0, base=0,
                               pattern=[[-1, P]], channel_multiplier=1).then_inc(ident_ready, 1)
            pool.wait_ge(weights_in, 16 * N_WEIGHT_DMAS)

            def over_tiles(row):
                return row[:, :].unsqueeze(1).broadcast_to([P, TILES, P])

            def node_step(i):
                g = i + -1
                if g.inside(NG):
                    s = g.slot % 2
                    pool.wait_ge(N["that"], g.done)
                    pool.tensor_tensor(tiles(scaled2[s]), tiles(that2[s]), over_tiles(gamma_b), ALU.mult
                                       ).then_inc(N["scaled"], 1)
                g = i
                if g.inside(NG):
                    pool.wait_ge(n_x_in[g.slot], g.landed)
                    if (g + -2).inside(NG):
                        pool.wait_ge(N["x1"], (g + -2).done)
                    pool.tensor_tensor(tiles(xb2[g.slot % 2]), tiles(A4[g.slot]), over_tiles(beta_b), ALU.add
                                       ).then_inc(N["xb"], 1)

            steps(pool, node_step, *N_STEPS, N_LOOP)

            def edge_step(i, layer):
                S, n = E, done_by(layer)
                table = x if layer == 0 else x1
                result = x1 if layer == 0 else out
                g = i + -2
                if layer == 0 and g.inside(EG):
                    s = g.slot % 2
                    pool.wait_ge(S["that"], n(g))
                    pool.tensor_tensor(tiles(scaled2[s]), tiles(that2[s]), over_tiles(gamma_b), ALU.mult
                                       ).then_inc(S["scaled"], 1)
                g = i + 3
                if g.inside(EG):
                    waits = [(e_idx_in[layer][g.slot], g.landed * (2 - layer))]
                    if (g + -4).inside(EG):
                        waits += [(S["xsn"], n(g + -4)), (S["xdn"], n(g + -4)), (S["xb"], n(g + -4))]
                    wait_all(pool, waits)
                    for j in range(TILES):
                        pool.indirect_dma_start(out=A4[g.slot][:, j * P:(j + 1) * P], out_offset=None, in_=table,
                                                in_offset=bass.IndirectOffsetOnAxis(ap=srcidx[g.slot][:, j:j + 1], axis=0)
                                                ).then_inc(e_src_in[layer][g.slot], 16)
                        if layer == 0:
                            pool.indirect_dma_start(out=B4[g.slot][:, j * P:(j + 1) * P], out_offset=None, in_=table,
                                                    in_offset=bass.IndirectOffsetOnAxis(ap=dstidx[g.slot][:, j:j + 1], axis=0)
                                                    ).then_inc(e_dst_in[layer][g.slot], 16)
                g = i + 1
                if g.inside(EG):
                    pool.wait_ge(e_dst_in[layer][g.slot], g.landed * (TILES if layer == 0 else 1))
                    if (g + -4).inside(EG):
                        pool.wait_ge(S["new"], n(g + -4))
                    pool.tensor_tensor(tiles(E4[g.slot]), tiles(B4[g.slot]), over_tiles(beta_b if layer == 0 else b2b_b),
                                       ALU.add).then_inc(S["xb"], 1)
                g = i + -3
                if g.inside(EG):
                    wait_all(pool, [(S["new"], n(g)), (e_outidx_in[layer][g.slot], g.landed)])
                    for j in range(TILES):
                        pool.indirect_dma_start(out=result, in_=F4[g.slot][:, j * P:(j + 1) * P], in_offset=None,
                                                out_offset=bass.IndirectOffsetOnAxis(ap=outidx[g.slot][:, j:j + 1], axis=0),
                                                bounds_check=n_nodes - 1, oob_is_err=False
                                                ).then_inc(e_scattered[layer][g.slot], 16)

            nodes_are_done(pool)
            steps(pool, lambda i: edge_step(i, 0), *E_STEPS, E_LOOP)
            edges0_are_done(pool)
            steps(pool, lambda i: edge_step(i, 1), *E_STEPS, E_LOOP)


def kernel(**inputs):
    import numpy as np
    import concourse.bacc as bacc
    from concourse.bass_utils import run_bass_kernel_spmd

    a = {k: np.ascontiguousarray(v) for k, v in inputs.items()}
    n_edges = a["src"].shape[0]
    groups = -(-n_edges // GROUP)
    pad = groups * GROUP - n_edges

    def padded(v, fill):
        return np.concatenate([v, np.full((pad,) + v.shape[1:], fill, v.dtype)])

    def columns(v):
        return np.ascontiguousarray(v.reshape(groups, TILES, P).transpose(0, 2, 1))

    dst, none = a["dst"], np.full(1, -1, a["dst"].dtype)
    arrays = {
        "x": a["x"],
        "edge_attr": padded(a["edge_attr_128"], 0),
        "src_cols": columns(padded(a["src"], 0)),
        "dst_cols": columns(padded(dst, 0)),
        "next_cols": columns(padded(np.concatenate([dst[1:], none]), 0)),
        "dst_rows": padded(dst, -1).reshape(groups, GROUP),
        "prev_rows": padded(np.concatenate([none, dst[:-1]]), -2).reshape(groups, GROUP),
    }
    for k in ("msg_W1", "msg_b1", "msg_W2", "msg_b2", "upd_W1", "upd_b1", "upd_W2", "upd_b2", "ln_gamma", "ln_beta"):
        arrays[k] = a["L0_gnn_" + k]
    for k in ("u", "W1a", "b1a", "W1b", "b1b", "W2a", "b2a", "W2b", "b2b"):
        arrays["glob_u" if k == "u" else k] = a["L1_gnn_" + k]

    nc = bacc.Bacc("TRN2", target_bir_lowering=False, num_devices=1)
    aps = {k: nc.dram_tensor(k, v.shape, mybir.dt.from_np(v.dtype), kind="ExternalInput").ap() for k, v in arrays.items()}
    out = nc.dram_tensor("out", a["x"].shape, F32, kind="ExternalOutput").ap()
    build(nc, **aps, out=out)
    r = run_bass_kernel_spmd(nc, [arrays], core_ids=[0])
    return r.results[0]["out"]
```

```python
from contextlib import ExitStack

import concourse.bass as bass
from concourse import mybir

F32 = mybir.dt.float32
BF16 = mybir.dt.bfloat16
I32 = mybir.dt.int32
ALU = mybir.AluOpType
ACT = mybir.ActivationFunctionType

P = 128
TILES = 4
GROUP = TILES * P
LN_EPS = 1e-5
NO_ROW = 1 << 20


class At:

    def __init__(self, turn, slot, per):
        self.turn, self.slot, self.per = turn, slot, per

    @staticmethod
    def number(i, per):
        return At(i // per, i % per, per)

    def __add__(self, lag):
        return At(self.turn + (self.slot + lag) // self.per, (self.slot + lag) % self.per, self.per)

    @property
    def index(self):
        return self.turn * self.per + self.slot

    @property
    def done(self):
        return self.turn * self.per + (self.slot + 1)

    def ring(self, n):
        return self.slot % n

    def uses(self, n, each=1):
        return self.turn * (self.per // n * each) + (self.slot // n + 1) * each

    def inside(self, groups):
        return not isinstance(self.turn, int) or 0 <= self.index < groups

    def quarter(self):
        return self.slot % 4, At(self.turn, self.slot // 4, self.per // 4)


def steps(eng, body, first, end, loop_turns, per):
    a, b = loop_turns
    if b > a:
        for i in range(first, a * per):
            body(At.number(i, per))
        with eng.Fori(a, b) as turn:
            for slot in range(per):
                body(At(turn, slot, per))
    for i in range(b * per if b > a else first, end):
        body(At.number(i, per))


def ring_landed(g, n, dmas=1):
    return g.uses(n, 16 * dmas)


def build(nc, x, edge_attr_T, src_cols, dst_cols, next_cols, dst_rows, prev_rows,
          msg_W1, msg_b1, msg_W2, msg_b2, upd_W1, upd_b1, upd_W2, upd_b2, ln_gamma, ln_beta,
          glob_u, W1a, b1a, W1b, b1b, W2a, b2a, W2b, b2b, out):
    n_nodes, D = x.shape
    NG = -(-n_nodes // GROUP)
    EG = src_cols.shape[0]
    n_edges = EG * GROUP
    assert D == P and NG > 12 and EG >= 8

    x1 = nc.dram_tensor("x1_scratch", [n_nodes, D], F32, kind="Internal").ap()
    x1_edge = nc.dram_tensor("x1_edge_scratch", [n_edges, D], F32, kind="Internal").ap()
    same_d = nc.dram_tensor("same_scratch", [EG, GROUP], F32, kind="Internal").ap()
    rcount_d = nc.dram_tensor("rcount_scratch", [EG, GROUP], F32, kind="Internal").ap()
    rowidx_d = nc.dram_tensor("rowidx_scratch", [EG, P, TILES], I32, kind="Internal").ap()
    carry_d = nc.dram_tensor("carry_scratch", [3, EG + 1], F32, kind="Internal").ap()

    ctx = ExitStack()
    with ctx:
        def sb(name, shape, dt=F32):
            return ctx.enter_context(nc.sbuf_tensor(name, shape, dt))

        def sem(name):
            return ctx.enter_context(nc.semaphore(name))

        def sems(prefix, names):
            return {n: sem(f"{prefix}_{n}") for n in names.split()}

        def slot_sems(name, n):
            return [sem(f"{name}{k}") for k in range(n)]

        ident = sb("ident", [P, P])
        eps = sb("eps", [P, 1])
        gamma_b = sb("gamma_b", [P, P])
        beta_b = sb("beta_b", [P, P])
        b2b_b = sb("b2b_b", [P, P])
        msg_W1s = sb("msg_W1s", [P, 3, P])
        msg_W2s = sb("msg_W2s", [P, 1, P])
        upd_W1s = sb("upd_W1s", [P, 2, P])
        upd_W2s = sb("upd_W2s", [P, 1, P])
        W1as = sb("W1as", [P, 2, 2 * P])
        W1bs = sb("W1bs", [P, 2, P])
        W2as = sb("W2as", [P, 3, 2 * P])
        W2bs = sb("W2bs", [P, 2, P])
        cols = sb("cols", [P, 10])
        MSG_B1, MSG_B2, UPD_B1, B1A, B1B, B2A, GLOB = 0, 1, 2, 3, 5, 6, 8
        b2a_full = sb("b2a_full", [P, 2])
        ones3 = sb("ones3", [3, P], BF16)
        bias_f = sb("bias_f", [1, 2, P])
        bias_rest = sb("bias_rest", [1, 2, 2, P])
        bias_parts = sb("bias_parts", [1, 3, 2, GROUP], BF16)
        bias_rows = sb("bias_rows", [3, 2, GROUP], BF16)
        UPD_B2, B2B = 0, 1
        dstc = sb("dstc", [P, EG, TILES], I32)
        nextc = sb("nextc", [P, EG, TILES], I32)
        samec = sb("samec", [P, EG, TILES])
        rowidx = sb("rowidx", [P, EG, TILES], I32)
        ends = sb("ends", [1, 2, EG])
        carries = sb("carries", [1, EG + 1])
        carry_in = sb("carry_in", [EG, 1])

        big = [P, GROUP]
        n_taken = [0]
        room = [sb(f"room{k}", big) for k in range(62)]

        def take(n):
            n_taken[0] += n
            return room[n_taken[0] - n:n_taken[0]]

        (dstr, prevr, samer, ones_r, zeros_r, count, through, count2, count3, rcount) = [
            room[40 + k][0:EG, :].bitcast(I32) if k < 2 else room[40 + k][0:EG, :] for k in range(10)]

        n_x, n_xn, n_x1 = take(4), take(4), take(8)
        n_out, n_x1n = take(2), take(2)
        n_t, n_that, n_scaled, n_xb = take(2), take(2), take(2), take(2)
        n_hT, n_uT, n_h1T, n_v0T, n_v1T = take(2), take(2), take(2), take(2), take(2)
        a_xs, a_xd, a_xsn, a_xdn, a_xb = take(2), take(2), take(1), take(2), take(2)
        a_attrT, a_sT, a_dT = take(2), take(1), take(2)
        a_mT, a_zT, a_sum, a_uT = take(1), take(1), take(2), take(1)
        a_t, a_that, a_scaled, a_new, a_same = take(1), take(1), take(1), take(1), take(1)
        n_taken[0] = 0
        p_rows = take(4)
        b_xs, b_xd, b_xb, b_new = take(4), take(4), take(4), take(4)
        b_xsn, b_xdn, b_attrT, b_sT, b_dT = take(2), take(2), take(2), take(2), take(2)
        b_mT, b_uT = [take(2), take(2)], [take(2), take(2)]
        b_zT, b_sum, b_agg, b_same, b_rcount = take(2), take(2), take(2), take(2), take(2)

        srcidx = [sb(f"srcidx_{k}", [P, TILES], I32) for k in range(4)]
        dstidx = [sb(f"dstidx_{k}", [P, TILES], I32) for k in range(2)]
        outidx = [sb(f"outidx_{k}", [P, TILES], I32) for k in range(4)]

        class Norms:

            def __init__(self, name):
                def two(what, *shape):
                    return [sb(f"{name}_{what}{k}", [P, 12, *shape]) for k in range(2)]
                self.stats = two("stats", 6)
                self.both, self.diff, self.sq = two("both"), two("diff"), two("sq")
                self.mean, self.sumsq, self.sd, self.rstd, self.shift = (
                    two("mean"), two("sumsq"), two("sd"), two("rstd"), two("shift"))

        node_norms, edge_norms = Norms("nn"), Norms("en")

        bank = [ctx.enter_context(nc.psum_tensor(f"bank{k}", big, F32)) for k in range(8)]
        hT_ps, v0_ps, v1_ps, o_ps, d_ps = bank[0:5]
        a_ps = bank[5:8]

        weights_in, bias_cols_in, edge_lists_in, bias_rows_in = map(
            sem, ("weights_in", "bias_cols_in", "edge_lists_in", "bias_rows_in"))
        ident_ready, const_ready, bias_chain, glob_ready, b2a_ready, norms_clear = map(
            sem, ("ident_ready", "const_ready", "bias_chain", "glob_ready", "b2a_ready", "norms_clear"))
        L = sems("lists", "idx idx_out same count ends_out ends_in carry carry_out carry_in rcount rcount_out")
        N = sems("n", "stats link var sd norms xn hT_ps hT u_ps uT d_ps t that scaled xb x1 "
                      "x1n h1T_ps h1T v0_ps v1_ps v0T v1T o_ps out")
        n_x_in, n_x1_stored, n_out_stored = slot_sems("n_x_in", 4), slot_sems("n_x1_stored", 8), slot_sems("n_out_stored", 2)
        A = sems("a", "stats t_stats link var sd norms xsn xdn s_ps d_ps sT dT m_ps mT z_ps zT sum u_ps uT o_ps xb t that scaled new")
        a_idx_in, a_xs_in, a_xd_in, a_attr_in = (slot_sems(f"a_{w}_in", 2) for w in ("idx", "xs", "xd", "attr"))
        a_same_in, a_stored = slot_sems("a_same_in", 1), slot_sems("a_stored", 1)
        p_rows_in, p_scattered = slot_sems("p_rows_in", 4), slot_sems("p_scattered", 4)
        B = sems("b", "stats link var sd norms xsn xdn s_ps d_ps sT dT m_ps mT z_ps zT sum agg u_ps uT o_ps xb new")
        b_src_in, b_scattered, b_outidx_in = (slot_sems(f"b_{w}", 4) for w in ("src_in", "scattered", "outidx_in"))
        b_idx_in, b_xd_in, b_attr_in, b_same_in = (slot_sems(f"b_{w}_in", n) for w, n in (("idx", 4), ("xd", 4), ("attr", 2), ("same", 2)))

        N_WEIGHT_DMAS = 11
        N_COL_DMAS = 11

        A_STEPS = (-8, max(NG + 9, 4 * (EG + 2)))
        A_LOOP = (2, min((NG - 4) // 8, (EG - 2) // 2))
        P_STEPS, P_LOOP = (0, EG + 1), (1, EG // 4)
        B_STEPS, B_LOOP = (-4, EG + 3), (1, (EG - 4) // 4)

        def all_landed(eng, slots, groups, dmas=1):
            for k, s in enumerate(slots):
                eng.wait_ge(s, 16 * dmas * len(range(k, groups, len(slots))))

        def first_phase_done(eng):
            eng.wait_ge(N["out"], NG)
            eng.wait_ge(A["new"], EG)
            all_landed(eng, n_x1_stored, NG)
            all_landed(eng, n_out_stored, NG)
            all_landed(eng, a_stored, EG)

        def patch_done(eng):
            all_landed(eng, p_scattered, EG, TILES)

        def wait_all(eng, pairs):
            for _, count_ in pairs:
                if not isinstance(count_, int):
                    eng.lower_val(count_)
            eng.wait_ge(ident_ready, 2)
            for semaphore, count_ in pairs:
                eng.wait_ge(semaphore, count_)

        def last_group(g):
            return isinstance(g.turn, int) and g.index == NG - 1

        def node_rows(t, g):
            rows = t[n_nodes - GROUP:n_nodes, :] if last_group(g) else t[bass.ds(g.index * GROUP, GROUP), :]
            return rows.rearrange("(p j) f -> p (j f)", p=P)

        def edge_rows(t, g):
            return t[bass.ds(g.index * GROUP, GROUP), :].rearrange("(j p) f -> p j f", p=P)

        def tiles(t):
            return t[:, :].rearrange("p (j f) -> p j f", j=TILES)

        def tile(t, j):
            return t[:, j * P:(j + 1) * P]

        def list_row(t, g):
            return t[bass.ds(g.index, 1), :].broadcast_to([P, GROUP])

        def idx_cols(t, g):
            return t[bass.ds(g.index, 1), :, :].rearrange("o p j -> (o p) j")

        block = ctx.enter_context(nc.Block())

        @block.sync
        def _(sp):
            for col, src, k in ((MSG_B1, msg_b1, 1), (MSG_B2, msg_b2, 1), (UPD_B1, upd_b1, 1), (B1A, b1a, 2),
                                (B1B, b1b, 1), (B2A, b2a, 2), (GLOB, glob_u[0, :], 1)):
                for h in range(k):
                    sp.dma_start(cols[:, col + h:col + h + 1],
                                 src[h * P:(h + 1) * P].rearrange("(p o) -> p o", o=1)).then_inc(bias_cols_in, 16)
            sp.dma_start(bias_f[:, UPD_B2, :], upd_b2.rearrange("(o f) -> o f", o=1)).then_inc(bias_cols_in, 16)
            sp.dma_start(bias_f[:, B2B, :], b2b.rearrange("(o f) -> o f", o=1)).then_inc(bias_cols_in, 16)
            for dst, src in ((gamma_b, ln_gamma), (beta_b, ln_beta), (b2b_b, b2b)):
                sp.dma_start(dst[:, :], src.rearrange("(o f) -> o f", o=1).broadcast_to([P, P])).then_inc(weights_in, 16)
            for dst, src in ((msg_W1s, msg_W1), (msg_W2s, msg_W2), (upd_W1s, upd_W1), (upd_W2s, upd_W2),
                             (W1as, W1a), (W1bs, W1b), (W2as, W2a), (W2bs, W2b)):
                sp.dma_start(dst[:, :, :], src.rearrange("(k p) n -> p k n", p=P)).then_inc(weights_in, 16)
            sp.dma_start(dstc[:, :, :], dst_cols.rearrange("g p j -> p g j")).then_inc(edge_lists_in, 16)
            sp.dma_start(nextc[:, :, :], next_cols.rearrange("g p j -> p g j")).then_inc(edge_lists_in, 16)
            sp.dma_start(dstr, dst_rows).then_inc(edge_lists_in, 16)
            sp.dma_start(prevr, prev_rows).then_inc(edge_lists_in, 16)
            sp.wait_ge(bias_chain, 8)
            for k in range(3):
                sp.dma_start(bias_rows[k:k + 1, :, :], bias_parts[:, k, :, :]).then_inc(bias_rows_in, 16)
            sp.wait_ge(L["idx"], 2)
            sp.dma_start(rowidx_d.rearrange("g p j -> p g j"), rowidx[:, :, :]).then_inc(L["idx_out"], 16)
            sp.wait_ge(L["same"], 1)
            sp.dma_start(same_d, samer).then_inc(L["idx_out"], 16)
            sp.wait_ge(L["count"], 2)
            sp.dma_start(carry_d[0:1, 0:EG].rearrange("o g -> g o"), count[:, GROUP - 1:GROUP]).then_inc(L["ends_out"], 16)
            sp.dma_start(carry_d[1:2, 0:EG].rearrange("o g -> g o"), through[:, GROUP - 1:GROUP]).then_inc(L["ends_out"], 16)
            sp.wait_ge(L["ends_out"], 32)
            sp.dma_start(ends[:, 0, :], carry_d[0:1, 0:EG]).then_inc(L["ends_in"], 16)
            sp.dma_start(ends[:, 1, :], carry_d[1:2, 0:EG]).then_inc(L["ends_in"], 16)
            sp.wait_ge(L["carry"], 2)
            sp.dma_start(carry_d[2:3, :], carries[:, :]).then_inc(L["carry_out"], 16)
            sp.wait_ge(L["carry_out"], 16)
            sp.dma_start(carry_in[:, :], carry_d[2:3, 0:EG].rearrange("o g -> g o")).then_inc(L["carry_in"], 16)
            sp.wait_ge(L["rcount"], 3)
            sp.dma_start(rcount_d, rcount).then_inc(L["rcount_out"], 16)
            sp.wait_ge(L["idx_out"], 32)
            sp.wait_ge(L["rcount_out"], 16)

            def step(i):
                g = i + 3
                if g.inside(NG):
                    if (g + -4).inside(NG):
                        sp.wait_ge(N["xb"], (g + -4).done)
                        sp.wait_ge(N["xn"], (g + -4).done)
                    sp.dma_start(n_x[g.ring(4)][:, :], node_rows(x, g)).then_inc(n_x_in[g.ring(4)], 16)
                q, e = i.quarter()
                f = e + 2
                if q == 0 and f.inside(EG):
                    r = f.ring(2)
                    if (f + -2).inside(EG):
                        sp.wait_ge(a_xs_in[r], ring_landed(f + -2, 2, TILES))
                        sp.wait_ge(a_xd_in[r], ring_landed(f + -2, 2, TILES))
                    sp.dma_start(srcidx[r][:, :], idx_cols(src_cols, f)).then_inc(a_idx_in[r], 16)
                    sp.dma_start(dstidx[r][:, :], idx_cols(dst_cols, f)).then_inc(a_idx_in[r], 16)
                f = e
                if q == 1 and f.inside(EG):
                    if (f + -1).inside(EG):
                        sp.wait_ge(A["sum"], (f + -1).done)
                    sp.dma_start(a_same[0][:, :], list_row(same_d, f)).then_inc(a_same_in[0], 16)
                f = e + -2
                if q == 2 and f.inside(EG):
                    sp.wait_ge(A["new"], f.done)
                    sp.dma_start(edge_rows(x1_edge, f), tiles(a_new[0])).then_inc(a_stored[0], 16)
                f = e + 1
                if q == 3 and f.inside(EG):
                    r = f.ring(2)
                    if (f + -2).inside(EG):
                        sp.wait_ge(A["m_ps"], (f + -2).done)
                    sp.dma_start(a_attrT[r][:, :], edge_attr_T[:, bass.ds(f.index * GROUP, GROUP)]).then_inc(a_attr_in[r], 16)
                g = i + -3
                if g.inside(NG):
                    sp.wait_ge(N["x1"], g.done)
                    if last_group(g):
                        p = g + -1
                        sp.wait_ge(n_x1_stored[p.ring(8)], ring_landed(p, 8))
                    sp.dma_start(node_rows(x1, g), n_x1[g.ring(8)][:, :]).then_inc(n_x1_stored[g.ring(8)], 16)
                g = i + -8
                if g.inside(NG):
                    sp.wait_ge(N["out"], g.done)
                    if last_group(g):
                        p = g + -1
                        sp.wait_ge(n_out_stored[p.ring(2)], ring_landed(p, 2))
                    sp.dma_start(node_rows(out, g), n_out[g.ring(2)][:, :]).then_inc(n_out_stored[g.ring(2)], 16)

            steps(sp, step, *A_STEPS, A_LOOP, 8)

            def patch_step(i):
                g = i
                if g.inside(EG):
                    r = g.ring(4)
                    if (g + -4).inside(EG):
                        wait_all(sp, [(p_scattered[r], ring_landed(g + -4, 4, TILES))])
                    sp.dma_start(tiles(p_rows[r]), edge_rows(x1_edge, g)).then_inc(p_rows_in[r], 16)
                    sp.dma_start(outidx[r][:, :], idx_cols(rowidx_d, g)).then_inc(p_rows_in[r], 16)

            first_phase_done(sp)
            steps(sp, patch_step, *P_STEPS, P_LOOP, 4)

            def edge_step(i):
                g = i + 4
                if g.inside(EG):
                    r = g.ring(4)
                    if (g + -4).inside(EG):
                        sp.wait_ge(b_src_in[r], ring_landed(g + -4, 4, TILES))
                    sp.dma_start(srcidx[r][:, :], idx_cols(src_cols, g)).then_inc(b_idx_in[r], 16)
                g = i + 3
                if g.inside(EG):
                    r = g.ring(4)
                    if (g + -4).inside(EG):
                        sp.wait_ge(B["xb"], (g + -4).done)
                        sp.wait_ge(B["xdn"], (g + -4).done)
                    sp.dma_start(tiles(b_xd[r]), edge_rows(x1_edge, g)).then_inc(b_xd_in[r], 16)
                g = i + 1
                if g.inside(EG):
                    r = g.ring(2)
                    if (g + -2).inside(EG):
                        wait_all(sp, [(B["m_ps"], (g + -2).done)])
                    sp.dma_start(b_attrT[r][:, :], edge_attr_T[:, bass.ds(g.index * GROUP, GROUP)]).then_inc(b_attr_in[r], 16)
                g = i
                if g.inside(EG):
                    r = g.ring(2)
                    if (g + -2).inside(EG):
                        wait_all(sp, [(B["agg"], (g + -2).done)])
                    sp.dma_start(b_same[r][:, :], list_row(same_d, g)).then_inc(b_same_in[r], 16)
                    sp.dma_start(b_rcount[r][:, :], list_row(rcount_d, g)).then_inc(b_same_in[r], 16)
                    r = g.ring(4)
                    if (g + -4).inside(EG):
                        sp.wait_ge(b_scattered[r], ring_landed(g + -4, 4, TILES))
                    sp.dma_start(outidx[r][:, :], idx_cols(rowidx_d, g)).then_inc(b_outidx_in[r], 16)

            patch_done(sp)
            steps(sp, edge_step, *B_STEPS, B_LOOP, 4)
            all_landed(sp, b_scattered, EG, TILES)

        @block.tensor
        def _(pe):
            def transpose4(ps, src):
                for j in range(TILES):
                    last = pe.transpose(tile(ps, j), tile(src, j), ident[:, :])
                return last

            def product(ps, weights, h, parts):
                for k, (row, part) in enumerate(parts):
                    last = pe.matmul(ps[:, :], weights[:, row, h * P:(h + 1) * P], part[:, :],
                                     start=(k == 0), stop=(k == len(parts) - 1))
                return last

            def rows_product(ps, bias, parts, weights):
                if bias is not None:
                    pe.matmul(ps[:, :], ones3[:, :], bias_rows[:, bias, :], start=True, stop=False)
                for j in range(TILES):
                    for h, part in enumerate(parts):
                        last_of = h == len(parts) - 1
                        last = pe.matmul(tile(ps, j), tile(part, j), weights[:, h, :], start=(bias is None and h == 0),
                                         stop=(last_of and (bias is None or j == TILES - 1)))
                return last

            pe.wait_ge(weights_in, 16 * N_WEIGHT_DMAS)
            pe.wait_ge(bias_cols_in, 16 * N_COL_DMAS)
            pe.wait_ge(ident_ready, 2)
            for h in range(2):
                last = pe.matmul(bank[0][:, h:h + 1], W2as[:, 2, h * P:(h + 1) * P], cols[:, GLOB:GLOB + 1],
                                 start=True, stop=True)
            last.then_inc(glob_ready, 1)
            pe.wait_ge(b2a_ready, 1)
            pe.wait_ge(const_ready, 1)
            pe.wait_ge(bias_rows_in, 48)

            def step(i):
                q, e = i.quarter()
                g = i + -6
                if g.inside(NG):
                    pe.wait_ge(N["h1T"], g.done)
                    product(v0_ps, W2as, 0, [(0, n_h1T[g.ring(2)])]).then_inc(N["v0_ps"], 1)
                    product(v1_ps, W2as, 1, [(0, n_h1T[g.ring(2)])]).then_inc(N["v1_ps"], 1)
                f = e + -1
                if q == 1 and f.inside(EG):
                    pe.wait_ge(A["sum"], f.done)
                    product(a_ps[2], upd_W1s, 0, [(0, a_dT[f.ring(2)]), (1, a_sum[f.ring(2)])]).then_inc(A["u_ps"], 1)
                if q == 2 and f.inside(EG):
                    pe.wait_ge(A["uT"], f.done)
                    rows_product(a_ps[2], UPD_B2, [a_uT[0]], upd_W2s).then_inc(A["o_ps"], 1)
                g = i + -5
                if g.inside(NG):
                    pe.wait_ge(N["x1n"], g.done)
                    pe.wait_ge(N["hT"], (i + 0).done if i.inside(NG) else NG)
                    transpose4(hT_ps, n_x1n[g.ring(2)]).then_inc(N["h1T_ps"], 1)
                g = i
                if g.inside(NG):
                    pe.wait_ge(N["hT"], g.done)
                    if (g + -6).inside(NG):
                        pe.wait_ge(N["v0T"], (g + -6).done)
                    product(v0_ps, upd_W1s, 0, [(0, n_hT[g.ring(2)])]).then_inc(N["u_ps"], 1)
                g = i + -6
                if g.inside(NG):
                    if (g + -1).inside(NG):
                        pe.wait_ge(N["out"], (g + -1).done)
                    pe.wait_ge(N["v0T"], g.done)
                    pe.wait_ge(N["v1T"], g.done)
                    rows_product(o_ps, B2B, [n_v0T[g.ring(2)], n_v1T[g.ring(2)]], W2bs).then_inc(N["o_ps"], 1)
                f = e
                if q == 2 and f.inside(EG):
                    pe.wait_ge(A["sT"], f.done)
                    pe.wait_ge(A["dT"], f.done)
                    pe.wait_ge(a_attr_in[f.ring(2)], ring_landed(f, 2))
                    product(a_ps[0], msg_W1s, 0, [(0, a_sT[0]), (1, a_dT[f.ring(2)]), (2, a_attrT[f.ring(2)])]
                            ).then_inc(A["m_ps"], 1)
                if q == 3 and f.inside(EG):
                    pe.wait_ge(A["mT"], f.done)
                    product(a_ps[1], msg_W2s, 0, [(0, a_mT[0])]).then_inc(A["z_ps"], 1)
                g = i + 1
                if g.inside(NG):
                    pe.wait_ge(N["xn"], g.done)
                    if (i + -5).inside(NG):
                        pe.wait_ge(N["h1T"], (i + -5).done)
                    transpose4(hT_ps, n_xn[g.ring(4)]).then_inc(N["hT_ps"], 1)
                g = i
                if g.inside(NG):
                    if (g + -1).inside(NG):
                        pe.wait_ge(N["t"], (g + -1).done)
                    pe.wait_ge(N["uT"], g.done)
                    rows_product(d_ps, UPD_B2, [n_uT[g.ring(2)]], upd_W2s).then_inc(N["d_ps"], 1)
                f = e
                if q == 1 and f.inside(EG):
                    pe.wait_ge(A["xsn"], f.done)
                    if (f + -1).inside(EG):
                        pe.wait_ge(A["zT"], (f + -1).done)
                    transpose4(a_ps[0], a_xsn[0]).then_inc(A["s_ps"], 1)
                    pe.wait_ge(A["xdn"], f.done)
                    transpose4(a_ps[1], a_xdn[f.ring(2)]).then_inc(A["d_ps"], 1)

            steps(pe, step, *A_STEPS, A_LOOP, 8)

            def edge_step(i):
                ta_ps, tb_ps, z_ps, d_ps = bank[0:4]
                m_ps, u_ps = bank[4:6], bank[6:8]
                g = i
                if g.inside(EG):
                    r = g.ring(2)
                    pe.wait_ge(B["sT"], g.done)
                    pe.wait_ge(b_attr_in[r], ring_landed(g, 2))
                    product(m_ps[0], W1as, 0, [(0, b_sT[r]), (1, b_attrT[r])])
                    product(m_ps[1], W1as, 1, [(0, b_sT[r]), (1, b_attrT[r])]).then_inc(B["m_ps"], 1)
                g = i + -1
                if g.inside(EG):
                    r = g.ring(2)
                    pe.wait_ge(B["dT"], g.done)
                    pe.wait_ge(B["agg"], g.done)
                    product(u_ps[0], W2as, 0, [(0, b_dT[r]), (1, b_agg[r])])
                    product(u_ps[1], W2as, 1, [(0, b_dT[r]), (1, b_agg[r])]).then_inc(B["u_ps"], 1)
                g = i
                if g.inside(EG):
                    r = g.ring(2)
                    pe.wait_ge(B["mT"], g.done)
                    product(z_ps, W1bs, 0, [(0, b_mT[0][r]), (1, b_mT[1][r])]).then_inc(B["z_ps"], 1)
                g = i + 1
                if g.inside(EG):
                    r = g.ring(2)
                    pe.wait_ge(B["xsn"], g.done)
                    transpose4(ta_ps, b_xsn[r]).then_inc(B["s_ps"], 1)
                    pe.wait_ge(B["xdn"], g.done)
                    transpose4(tb_ps, b_xdn[r]).then_inc(B["d_ps"], 1)
                g = i + -1
                if g.inside(EG):
                    r = g.ring(2)
                    if (g + -1).inside(EG):
                        pe.wait_ge(B["new"], (g + -1).done)
                    pe.wait_ge(B["uT"], g.done)
                    rows_product(d_ps, None, [b_uT[0][r], b_uT[1][r]], W2bs).then_inc(B["o_ps"], 1)

            first_phase_done(pe)
            patch_done(pe)
            steps(pe, edge_step, *B_STEPS, B_LOOP, 4)

        @block.scalar
        def _(act):
            def relu(out_, in_, bias=None):
                if bias is None:
                    return act.activation(out_[:, :], in_[:, :], ACT.Relu)
                return act.activation(out_[:, :], in_[:, :], ACT.Relu, bias=bias)

            def col(k):
                return cols[:, k:k + 1]

            def root(norms, r):
                return act.activation(norms.sd[r][:, :], norms.sumsq[r][:, :], ACT.Sqrt, bias=eps[:, :], scale=1.0 / D)

            def norm(norms, r, stream, dst, src):
                for j in range(TILES):
                    c = stream * TILES + j
                    last = act.activation(tile(dst, j), tile(src, j), ACT.Identity,
                                          bias=norms.shift[r][:, c:c + 1], scale=norms.rstd[r][:, c:c + 1])
                return last

            act.wait_ge(const_ready, 1)
            act.wait_ge(bias_cols_in, 16 * N_COL_DMAS)
            act.wait_ge(b2a_ready, 1)

            def step(i):
                q, e = i.quarter()
                g = i + -6
                if g.inside(NG):
                    act.wait_ge(N["v0_ps"], g.done)
                    relu(n_v0T[g.ring(2)], v0_ps, b2a_full[:, 0:1]).then_inc(N["v0T"], 1)
                    act.wait_ge(N["v1_ps"], g.done)
                    relu(n_v1T[g.ring(2)], v1_ps, b2a_full[:, 1:2]).then_inc(N["v1T"], 1)
                f = e + -1
                if q == 1 and f.inside(EG):
                    act.wait_ge(A["u_ps"], f.done)
                    relu(a_uT[0], a_ps[2], col(UPD_B1)).then_inc(A["uT"], 1)
                g = i + -5
                if g.inside(NG):
                    act.wait_ge(N["h1T_ps"], g.done)
                    relu(n_h1T[g.ring(2)], hT_ps).then_inc(N["h1T"], 1)
                g = i
                if g.inside(NG):
                    act.wait_ge(N["u_ps"], g.done)
                    relu(n_uT[g.ring(2)], v0_ps, col(UPD_B1)).then_inc(N["uT"], 1)
                b = i + 1
                if b.inside(NG + 5):
                    act.wait_ge(N["norms"], b.done)
                g = i + -2
                if g.inside(NG):
                    if (g + -2).inside(NG):
                        act.wait_ge(N["scaled"], (g + -2).done)
                    norm(node_norms, b.ring(2), 1, n_that[g.ring(2)], n_t[g.ring(2)]).then_inc(N["that"], 1)
                g = i + -4
                if g.inside(NG):
                    if (g + -2).inside(NG):
                        act.wait_ge(N["h1T_ps"], (g + -2).done)
                    norm(node_norms, b.ring(2), 2, n_x1n[g.ring(2)], n_x1[g.ring(8)]).then_inc(N["x1n"], 1)
                b = i + 2
                if b.inside(NG + 5):
                    act.wait_ge(N["var"], b.done)
                    root(node_norms, b.ring(2)).then_inc(N["sd"], 1)
                g = i + 1
                if g.inside(NG):
                    act.wait_ge(N["hT_ps"], g.done)
                    relu(n_hT[g.ring(2)], hT_ps).then_inc(N["hT"], 1)
                f = e
                if q == 2 and f.inside(EG):
                    act.wait_ge(A["m_ps"], f.done)
                    relu(a_mT[0], a_ps[0], col(MSG_B1)).then_inc(A["mT"], 1)
                if q == 3 and f.inside(EG):
                    act.wait_ge(A["z_ps"], f.done)
                    if (f + -1).inside(EG):
                        act.wait_ge(A["sum"], (f + -1).done)
                    act.activation(a_zT[0][:, :], a_ps[1][:, :], ACT.Identity, bias=col(MSG_B2)).then_inc(A["zT"], 1)
                f = e + -2
                if q == 0 and f.inside(EG):
                    act.wait_ge(A["norms"], e.done)
                    if (f + -1).inside(EG):
                        act.wait_ge(A["scaled"], (f + -1).done)
                    norm(edge_norms, e.ring(2), 2, a_that[0], a_t[0]).then_inc(A["that"], 1)
                b = e + 1
                if q == 3 and b.inside(EG + 2):
                    act.wait_ge(A["var"], b.done)
                    root(edge_norms, b.ring(2)).then_inc(A["sd"], 1)
                f = e
                if q == 1 and f.inside(EG):
                    act.wait_ge(A["s_ps"], f.done)
                    relu(a_sT[0], a_ps[0]).then_inc(A["sT"], 1)
                    act.wait_ge(A["d_ps"], f.done)
                    relu(a_dT[f.ring(2)], a_ps[1]).then_inc(A["dT"], 1)

            steps(act, step, *A_STEPS, A_LOOP, 8)

            def edge_step(i):
                ta_ps, tb_ps, z_ps, d_ps = bank[0:4]
                m_ps, u_ps = bank[4:6], bank[6:8]
                g = i
                if g.inside(EG):
                    r = g.ring(2)
                    act.wait_ge(B["m_ps"], g.done)
                    relu(b_mT[0][r], m_ps[0], col(B1A))
                    relu(b_mT[1][r], m_ps[1], col(B1A + 1)).then_inc(B["mT"], 1)
                g = i + -1
                if g.inside(EG):
                    r = g.ring(2)
                    act.wait_ge(B["u_ps"], g.done)
                    relu(b_uT[0][r], u_ps[0], b2a_full[:, 0:1])
                    relu(b_uT[1][r], u_ps[1], b2a_full[:, 1:2]).then_inc(B["uT"], 1)
                g = i
                if g.inside(EG):
                    r = g.ring(2)
                    act.wait_ge(B["z_ps"], g.done)
                    if (g + -2).inside(EG):
                        act.wait_ge(B["sum"], (g + -2).done)
                    act.activation(b_zT[r][:, :], z_ps[:, :], ACT.Identity, bias=col(B1B)).then_inc(B["zT"], 1)
                g = i + 2
                if g.inside(EG):
                    act.wait_ge(B["var"], g.done)
                    root(edge_norms, g.ring(2)).then_inc(B["sd"], 1)
                g = i + 1
                if g.inside(EG):
                    r = g.ring(2)
                    act.wait_ge(B["s_ps"], g.done)
                    relu(b_sT[r], ta_ps).then_inc(B["sT"], 1)
                    act.wait_ge(B["d_ps"], g.done)
                    relu(b_dT[r], tb_ps).then_inc(B["dT"], 1)

            first_phase_done(act)
            patch_done(act)
            steps(act, edge_step, *B_STEPS, B_LOOP, 4)

        @block.vector
        def _(dve):
            def stats(norms, r, stream, src):
                for j in range(TILES):
                    last = dve.bn_stats(norms.stats[r][:, stream * TILES + j, :], tile(src, j))
                return last

            def variances(norms, r, link, n):
                s = norms.stats[r]
                dve.tensor_tensor(norms.both[r][:, :], s[:, :, 2], s[:, :, 5], ALU.add)
                dve.tensor_tensor(norms.diff[r][:, :], s[:, :, 1], s[:, :, 4], ALU.subtract).then_inc(link, 1)
                dve.wait_ge(link, 3 * n - 2)
                dve.scalar_tensor_tensor(out=norms.mean[r][:, :], in0=norms.diff[r][:, :], scalar=-0.5, in1=s[:, :, 1],
                                         op0=ALU.mult, op1=ALU.add)
                dve.scalar_tensor_tensor(out=norms.sq[r][:, :], in0=norms.diff[r][:, :], scalar=D / 4.0,
                                         in1=norms.diff[r][:, :], op0=ALU.mult, op1=ALU.mult).then_inc(link, 1)
                dve.wait_ge(link, 3 * n - 1)
                return dve.tensor_tensor(norms.sumsq[r][:, :], norms.sq[r][:, :], norms.both[r][:, :], ALU.add)

            def invert(norms, r, link, n):
                dve.reciprocal(norms.rstd[r][:, :], norms.sd[r][:, :]).then_inc(link, 1)
                dve.wait_ge(link, 3 * n)
                return dve.scalar_tensor_tensor(out=norms.shift[r][:, :], in0=norms.mean[r][:, :], scalar=-1.0,
                                                in1=norms.rstd[r][:, :], op0=ALU.mult, op1=ALU.mult)

            def norm(norms, r, stream, dst, src):
                for j in range(TILES):
                    c = stream * TILES + j
                    last = dve.tensor_scalar(tile(dst, j), tile(src, j), norms.mean[r][:, c:c + 1],
                                             norms.rstd[r][:, c:c + 1], ALU.subtract, ALU.mult)
                return last

            for norms in (node_norms, edge_norms):
                for r in range(2):
                    dve.memset(norms.stats[r][:, :, :], 0.0).then_inc(norms_clear, 1)
            dve.memset(eps[:, :], LN_EPS)
            dve.memset(ones3[:, :], 1.0)
            dve.memset(ones_r, 1.0)
            dve.memset(carries[:, :], 0.0)
            dve.memset(zeros_r, 0.0).then_inc(const_ready, 1)
            dve.wait_ge(const_ready, 1)
            dve.wait_ge(bias_cols_in, 16 * N_COL_DMAS)

            def wide(k):
                return bias_parts[:, k, :, :].rearrange("o b (j f) -> o b j f", j=TILES)

            rests = [bias_f[:, :, :], bias_rest[:, 0, :, :], bias_rest[:, 1, :, :]]
            n = 0
            for k in range(3):
                for b in range(2):
                    dve.tensor_copy(wide(k)[:, b, :, :],
                                    rests[k][:, b, :].unsqueeze(1).broadcast_to([1, TILES, P])).then_inc(bias_chain, 1)
                n += 2
                dve.wait_ge(bias_chain, n)
                if k < 2:
                    dve.tensor_tensor(rests[k + 1], rests[k], wide(k)[:, :, 0, :], ALU.subtract).then_inc(bias_chain, 1)
                    n += 1
                    dve.wait_ge(bias_chain, n)
            dve.wait_ge(glob_ready, 1)
            dve.tensor_tensor(b2a_full[:, :], bank[0][:, 0:2], cols[:, B2A:B2A + 2], ALU.add).then_inc(b2a_ready, 1)
            dve.wait_ge(edge_lists_in, 64)
            dve.tensor_tensor(samec[:, :, :], dstc[:, :, :], nextc[:, :, :], ALU.is_equal).then_inc(L["idx"], 1)
            dve.wait_ge(L["idx"], 1)
            dve.scalar_tensor_tensor(out=rowidx[:, :, :], in0=samec[:, :, :], scalar=float(NO_ROW), in1=dstc[:, :, :],
                                     op0=ALU.mult, op1=ALU.add).then_inc(L["idx"], 1)
            dve.tensor_tensor(samer, dstr, prevr, ALU.is_equal).then_inc(L["same"], 1)
            dve.wait_ge(L["same"], 1)
            dve.tensor_tensor_scan(count, samer, ones_r, 0.0, ALU.mult, ALU.add).then_inc(L["count"], 1)
            dve.tensor_tensor_scan(through, samer, zeros_r, 1.0, ALU.mult, ALU.add).then_inc(L["count"], 1)
            dve.wait_ge(L["ends_in"], 32)
            dve.tensor_tensor_scan(carries[:, 1:EG + 1], ends[:, 1, :], ends[:, 0, :], 0.0, ALU.mult, ALU.add
                                   ).then_inc(L["carry"], 2)
            dve.wait_ge(L["carry_in"], 16)
            dve.scalar_tensor_tensor(out=count2, in0=through, scalar=carry_in[:, 0:1], in1=count,
                                     op0=ALU.mult, op1=ALU.add).then_inc(L["rcount"], 1)
            dve.wait_ge(L["rcount"], 1)
            dve.tensor_scalar(count3, count2, 1.0, None, ALU.max).then_inc(L["rcount"], 1)
            dve.wait_ge(L["rcount"], 2)
            dve.reciprocal(rcount, count3).then_inc(L["rcount"], 1)
            dve.wait_ge(norms_clear, 4)
            dve.wait_ge(L["idx_out"], 32)
            dve.wait_ge(L["rcount_out"], 16)

            def step(i):
                q, e = i.quarter()
                b = i + 1
                if b.inside(NG + 5):
                    dve.wait_ge(N["sd"], b.done)
                    invert(node_norms, b.ring(2), N["link"], b.done).then_inc(N["norms"], 1)
                g = i + 1
                if g.inside(NG):
                    norm(node_norms, b.ring(2), 0, n_xn[g.ring(4)], n_x[g.ring(4)]).then_inc(N["xn"], 1)
                if q == 0 and e.inside(EG + 2):
                    dve.wait_ge(A["sd"], e.done)
                    invert(edge_norms, e.ring(2), A["link"], e.done).then_inc(A["norms"], 1)
                if q == 1 and e.inside(EG):
                    if (e + -1).inside(EG):
                        dve.wait_ge(A["s_ps"], (e + -1).done)
                    norm(edge_norms, e.ring(2), 0, a_xsn[0], a_xs[e.ring(2)]).then_inc(A["xsn"], 1)
                    norm(edge_norms, e.ring(2), 1, a_xdn[e.ring(2)], a_xd[e.ring(2)]).then_inc(A["xdn"], 1)
                g = i + -7
                if g.inside(NG):
                    dve.wait_ge(N["o_ps"], g.done)
                    if (g + -2).inside(NG):
                        dve.wait_ge(n_out_stored[g.ring(2)], ring_landed(g + -2, 2))
                    dve.tensor_tensor(n_out[g.ring(2)][:, :], o_ps[:, :], n_x1[g.ring(8)][:, :], ALU.add
                                      ).then_inc(N["out"], 1)
                g = i + -1
                if g.inside(NG):
                    dve.wait_ge(N["d_ps"], g.done)
                    if (g + -2).inside(NG):
                        dve.wait_ge(N["that"], (g + -2).done)
                    dve.scalar_tensor_tensor(out=n_t[g.ring(2)][:, :], in0=n_xn[g.ring(4)][:, :], scalar=0.0,
                                             in1=d_ps[:, :], op0=ALU.max, op1=ALU.add).then_inc(N["t"], 1)
                f = e + -1
                if q == 0 and f.inside(EG):
                    dve.wait_ge(a_same_in[0], ring_landed(f, 1))
                    dve.wait_ge(A["zT"], f.done)
                    before = 0.0
                    if (f + -1).inside(EG):
                        dve.wait_ge(A["sum"], (f + -1).done)
                        before = a_sum[(f + -1).ring(2)][:, GROUP - 1:GROUP]
                    dve.tensor_tensor_scan(a_sum[f.ring(2)][:, :], a_same[0][:, :], a_zT[0][:, :], before,
                                           ALU.mult, ALU.add).then_inc(A["sum"], 1)
                b = i + 2
                r = b.ring(2)
                g, last = b, None
                if g.inside(NG):
                    dve.wait_ge(n_x_in[g.ring(4)], ring_landed(g, 4))
                    last = stats(node_norms, r, 0, n_x[g.ring(4)])
                g = i + -3
                if g.inside(NG):
                    dve.wait_ge(N["x1"], g.done)
                    last = stats(node_norms, r, 2, n_x1[g.ring(8)])
                g = i + -1
                if g.inside(NG):
                    dve.wait_ge(N["t"], g.done)
                    last = stats(node_norms, r, 1, n_t[g.ring(2)])
                if b.inside(NG + 5):
                    last.then_inc(N["stats"], 1)
                    dve.wait_ge(N["stats"], b.done)
                    variances(node_norms, r, N["link"], b.done).then_inc(N["var"], 1)
                eb = e + 1
                if q == 2 and eb.inside(EG):
                    dve.wait_ge(a_xs_in[eb.ring(2)], ring_landed(eb, 2, TILES))
                    stats(edge_norms, eb.ring(2), 0, a_xs[eb.ring(2)])
                    dve.wait_ge(a_xd_in[eb.ring(2)], ring_landed(eb, 2, TILES))
                    stats(edge_norms, eb.ring(2), 1, a_xd[eb.ring(2)]).then_inc(A["stats"], 1)
                f = e + -1
                if q == 3 and f.inside(EG):
                    dve.wait_ge(A["o_ps"], f.done)
                    dve.scalar_tensor_tensor(out=a_t[0][:, :], in0=a_xdn[f.ring(2)][:, :], scalar=0.0,
                                             in1=a_ps[2][:, :], op0=ALU.max, op1=ALU.add).then_inc(A["t"], 1)
                if q == 3 and eb.inside(EG + 2):
                    if f.inside(EG):
                        dve.wait_ge(A["t"], f.done)
                        stats(edge_norms, eb.ring(2), 2, a_t[0]).then_inc(A["t_stats"], 1)
                        dve.wait_ge(A["t_stats"], f.done)
                    if eb.inside(EG):
                        dve.wait_ge(A["stats"], eb.done)
                    variances(edge_norms, eb.ring(2), A["link"], eb.done).then_inc(A["var"], 1)

            steps(dve, step, *A_STEPS, A_LOOP, 8)

            def edge_step(i):
                d_ps = bank[3]
                g = i + -1
                if g.inside(EG):
                    r = g.ring(2)
                    dve.wait_ge(b_same_in[r], ring_landed(g, 2, 2))
                    dve.wait_ge(B["zT"], g.done)
                    before = 0.0
                    if (g + -1).inside(EG):
                        dve.wait_ge(B["sum"], (g + -1).done)
                        before = b_sum[1 - r][:, GROUP - 1:GROUP]
                    dve.tensor_tensor_scan(b_sum[r][:, :], b_same[r][:, :], b_zT[r][:, :], before, ALU.mult, ALU.add
                                           ).then_inc(B["sum"], 1)
                    dve.wait_ge(B["sum"], g.done)
                    dve.tensor_tensor(b_agg[r][:, :], b_sum[r][:, :], b_rcount[r][:, :], ALU.mult).then_inc(B["agg"], 1)
                g = i + 1
                if g.inside(EG):
                    dve.wait_ge(B["sd"], g.done)
                    r = g.ring(2)
                    invert(edge_norms, r, B["link"], g.done).then_inc(B["norms"], 1)
                    norm(edge_norms, r, 0, b_xsn[r], b_xs[g.ring(4)]).then_inc(B["xsn"], 1)
                    norm(edge_norms, r, 1, b_xdn[r], b_xd[g.ring(4)]).then_inc(B["xdn"], 1)
                g = i + 2
                if g.inside(EG):
                    r = g.ring(2)
                    dve.wait_ge(b_src_in[g.ring(4)], ring_landed(g, 4, TILES))
                    stats(edge_norms, r, 0, b_xs[g.ring(4)])
                    dve.wait_ge(b_xd_in[g.ring(4)], ring_landed(g, 4))
                    stats(edge_norms, r, 1, b_xd[g.ring(4)]).then_inc(B["stats"], 1)
                    dve.wait_ge(B["stats"], g.done)
                    variances(edge_norms, r, B["link"], g.done).then_inc(B["var"], 1)
                g = i + -2
                if g.inside(EG):
                    dve.wait_ge(B["o_ps"], g.done)
                    dve.wait_ge(B["xb"], g.done)
                    if (g + -4).inside(EG):
                        dve.wait_ge(b_scattered[g.ring(4)], ring_landed(g + -4, 4, TILES))
                    dve.tensor_tensor(b_new[g.ring(4)][:, :], d_ps[:, :], b_xb[g.ring(4)][:, :], ALU.add
                                      ).then_inc(B["new"], 1)

            first_phase_done(dve)
            patch_done(dve)
            steps(dve, edge_step, *B_STEPS, B_LOOP, 4)

        @block.gpsimd
        def _(pool):
            pool.memset(ident[:, :], 0.0).then_inc(ident_ready, 1)
            pool.wait_ge(ident_ready, 1)
            pool.affine_select(out=ident[:, :], in_=ident[:, :], compare_op=ALU.not_equal, fill=1.0, base=0,
                               pattern=[[-1, P]], channel_multiplier=1).then_inc(ident_ready, 1)
            pool.wait_ge(weights_in, 16 * N_WEIGHT_DMAS)
            pool.wait_ge(L["idx_out"], 32)
            pool.wait_ge(L["rcount_out"], 16)

            def over_tiles(dst, src, row, op):
                return pool.tensor_tensor(tiles(dst), tiles(src), row[:, :].unsqueeze(1).broadcast_to([P, TILES, P]), op)

            def gather(dst, table, idx, j, semaphore):
                pool.indirect_dma_start(out=tile(dst, j), out_offset=None, in_=table,
                                        in_offset=bass.IndirectOffsetOnAxis(ap=idx[:, j:j + 1], axis=0)
                                        ).then_inc(semaphore, 16)

            def scatter(table, idx, src, semaphore):
                for j in range(TILES):
                    pool.indirect_dma_start(out=table, in_=tile(src, j), in_offset=None,
                                            out_offset=bass.IndirectOffsetOnAxis(ap=idx[:, j:j + 1], axis=0),
                                            bounds_check=n_nodes - 1, oob_is_err=False).then_inc(semaphore, 16)

            def step(i):
                q, e = i.quarter()
                g = i + -2
                if g.inside(NG):
                    s = g.ring(2)
                    pool.wait_ge(N["that"], g.done)
                    over_tiles(n_scaled[s], n_that[s], gamma_b, ALU.mult).then_inc(N["scaled"], 1)
                    pool.wait_ge(N["scaled"], g.done)
                    if (g + -8).inside(NG):
                        pool.wait_ge(N["out"], (g + -8).done)
                        pool.wait_ge(n_x1_stored[g.ring(8)], ring_landed(g + -8, 8))
                    pool.tensor_tensor(n_x1[g.ring(8)][:, :], n_scaled[s][:, :], n_xb[s][:, :], ALU.add
                                       ).then_inc(N["x1"], 1)
                f = e + 2 if q else e + 1
                r = f.ring(2)
                if f.inside(EG):
                    first = q in (1, 3)
                    if first:
                        waits = [(a_idx_in[r], ring_landed(f, 2, 2))]
                        if (f + -2).inside(EG):
                            waits.append((A["xsn" if q == 1 else "xdn"], (f + -2).done))
                            if q == 3:
                                waits.append((A["xb"], (f + -2).done))
                        wait_all(pool, waits)
                    for j in ((0, 1) if first else (2, 3)):
                        if q in (1, 2):
                            gather(a_xs[r], x, srcidx[r], j, a_xs_in[r])
                        else:
                            gather(a_xd[r], x, dstidx[r], j, a_xd_in[r])
                if q == 2 and e.inside(EG):
                    pool.wait_ge(a_xd_in[e.ring(2)], ring_landed(e, 2, TILES))
                    if (e + -2).inside(EG):
                        pool.wait_ge(A["new"], (e + -2).done)
                    over_tiles(a_xb[e.ring(2)], a_xd[e.ring(2)], beta_b, ALU.add).then_inc(A["xb"], 1)
                f = e + -2
                if q == 1 and f.inside(EG):
                    pool.wait_ge(A["that"], f.done)
                    if (f + -1).inside(EG):
                        pool.wait_ge(A["new"], (f + -1).done)
                    over_tiles(a_scaled[0], a_that[0], gamma_b, ALU.mult).then_inc(A["scaled"], 1)
                    pool.wait_ge(A["scaled"], f.done)
                    if (f + -1).inside(EG):
                        pool.wait_ge(a_stored[0], ring_landed(f + -1, 1))
                    pool.tensor_tensor(a_new[0][:, :], a_scaled[0][:, :], a_xb[f.ring(2)][:, :], ALU.add
                                       ).then_inc(A["new"], 1)
                g = i
                if g.inside(NG):
                    pool.wait_ge(n_x_in[g.ring(4)], ring_landed(g, 4))
                    if (g + -2).inside(NG):
                        pool.wait_ge(N["x1"], (g + -2).done)
                    over_tiles(n_xb[g.ring(2)], n_x[g.ring(4)], beta_b, ALU.add).then_inc(N["xb"], 1)

            steps(pool, step, *A_STEPS, A_LOOP, 8)

            def patch_step(i):
                g = i + -1
                if g.inside(EG):
                    r = g.ring(4)
                    wait_all(pool, [(p_rows_in[r], ring_landed(g, 4, 2))])
                    scatter(x1, outidx[r], p_rows[r], p_scattered[r])

            first_phase_done(pool)
            steps(pool, patch_step, *P_STEPS, P_LOOP, 4)

            def edge_step(i):
                g = i + 3
                if g.inside(EG):
                    r = g.ring(4)
                    waits = [(b_idx_in[r], ring_landed(g, 4))]
                    if (g + -4).inside(EG):
                        waits.append((B["xsn"], (g + -4).done))
                    wait_all(pool, waits)
                    for j in range(TILES):
                        gather(b_xs[r], x1, srcidx[r], j, b_src_in[r])
                g = i + 1
                if g.inside(EG):
                    r = g.ring(4)
                    pool.wait_ge(b_xd_in[r], ring_landed(g, 4))
                    if (g + -4).inside(EG):
                        pool.wait_ge(B["new"], (g + -4).done)
                    over_tiles(b_xb[r], b_xd[r], b2b_b, ALU.add).then_inc(B["xb"], 1)
                g = i + -3
                if g.inside(EG):
                    r = g.ring(4)
                    wait_all(pool, [(B["new"], g.done), (b_outidx_in[r], ring_landed(g, 4))])
                    scatter(out, outidx[r], b_new[r], b_scattered[r])

            patch_done(pool)
            steps(pool, edge_step, *B_STEPS, B_LOOP, 4)


def kernel(**inputs):
    import numpy as np
    import concourse.bacc as bacc
    from concourse.bass_utils import run_bass_kernel_spmd

    a = {k: np.ascontiguousarray(v) for k, v in inputs.items()}
    n_edges = a["src"].shape[0]
    groups = -(-n_edges // GROUP)
    pad = groups * GROUP - n_edges

    def padded(v, fill):
        return np.concatenate([v, np.full((pad,) + v.shape[1:], fill, v.dtype)])

    def columns(v):
        return np.ascontiguousarray(v.reshape(groups, TILES, P).transpose(0, 2, 1))

    dst, none = a["dst"], np.full(1, -1, a["dst"].dtype)
    arrays = {
        "x": a["x"],
        "edge_attr_T": np.ascontiguousarray(padded(a["edge_attr_128"], 0).T),
        "src_cols": columns(padded(a["src"], 0)),
        "dst_cols": columns(padded(dst, 0)),
        "next_cols": columns(padded(np.concatenate([dst[1:], none]), 0)),
        "dst_rows": padded(dst, -1).reshape(groups, GROUP),
        "prev_rows": padded(np.concatenate([none, dst[:-1]]), -2).reshape(groups, GROUP),
    }
    for k in ("msg_W1", "msg_b1", "msg_W2", "msg_b2", "upd_W1", "upd_b1", "upd_W2", "upd_b2", "ln_gamma", "ln_beta"):
        arrays[k] = a["L0_gnn_" + k]
    for k in ("u", "W1a", "b1a", "W1b", "b1b", "W2a", "b2a", "W2b", "b2b"):
        arrays["glob_u" if k == "u" else k] = a["L1_gnn_" + k]

    nc = bacc.Bacc("TRN2", target_bir_lowering=False, num_devices=1)
    aps = {k: nc.dram_tensor(k, v.shape, mybir.dt.from_np(v.dtype), kind="ExternalInput").ap() for k, v in arrays.items()}
    out = nc.dram_tensor("out", a["x"].shape, F32, kind="ExternalOutput").ap()
    build(nc, **aps, out=out)
    r = run_bass_kernel_spmd(nc, [arrays], core_ids=[0])
    return r.results[0]["out"]
```

```python
from contextlib import ExitStack

import concourse.bass as bass
from concourse import mybir

F32 = mybir.dt.float32
BF16 = mybir.dt.bfloat16
I32 = mybir.dt.int32
ALU = mybir.AluOpType
ACT = mybir.ActivationFunctionType

P = 128
TILES = 4
GROUP = TILES * P
LN_EPS = 1e-5
NO_ROW = 1 << 20


class At:

    def __init__(self, turn, slot, per):
        self.turn, self.slot, self.per = turn, slot, per

    @staticmethod
    def number(i, per):
        return At(i // per, i % per, per)

    def __add__(self, lag):
        return At(self.turn + (self.slot + lag) // self.per, (self.slot + lag) % self.per, self.per)

    @property
    def index(self):
        return self.turn * self.per + self.slot

    @property
    def done(self):
        return self.turn * self.per + (self.slot + 1)

    def ring(self, n):
        return self.slot % n

    def uses(self, n, each=1):
        return self.turn * (self.per // n * each) + (self.slot // n + 1) * each

    def inside(self, groups):
        return not isinstance(self.turn, int) or 0 <= self.index < groups

    def quarter(self):
        return self.slot % 4, At(self.turn, self.slot // 4, self.per // 4)


def steps(eng, body, first, end, loop_turns, per):
    a, b = loop_turns
    if b > a:
        for i in range(first, a * per):
            body(At.number(i, per))
        with eng.Fori(a, b) as turn:
            for slot in range(per):
                body(At(turn, slot, per))
    for i in range(b * per if b > a else first, end):
        body(At.number(i, per))


def ring_landed(g, n, dmas=1):
    return g.uses(n, 16 * dmas)


def build(nc, x, edge_attr_T, src_cols, dst_cols, next_cols, dst_rows, prev_rows,
          bias_columns, bias_rows_f, free_rows, msg_W1, msg_W2, upd_W1, upd_W2, W1a, W1b, W2a, W2b, out):
    n_nodes, D = x.shape
    NG = -(-n_nodes // GROUP)
    EG = src_cols.shape[0]
    n_edges = EG * GROUP
    assert D == P and NG > 12 and EG >= 8

    x1_table = nc.dram_tensor("x1_scratch", [n_nodes + n_edges, D], F32, kind="Internal").ap()
    x1, x1_edge = x1_table[0:n_nodes, :], x1_table[n_nodes:n_nodes + n_edges, :]
    MAP_COLS = -(-n_nodes // P)
    row_map = nc.dram_tensor("row_map_scratch", [P * MAP_COLS, 1], I32, kind="Internal").ap()
    edge_row_d = nc.dram_tensor("edge_row_scratch", [EG, P, TILES], I32, kind="Internal").ap()
    src_row_d = nc.dram_tensor("src_row_scratch", [EG, P, TILES], I32, kind="Internal").ap()
    same_d = nc.dram_tensor("same_scratch", [EG, GROUP], F32, kind="Internal").ap()
    rcount_d = nc.dram_tensor("rcount_scratch", [EG, GROUP], F32, kind="Internal").ap()
    counts_d = nc.dram_tensor("counts_scratch", [2, EG, GROUP], BF16, kind="Internal").ap()
    rowidx_d = nc.dram_tensor("rowidx_scratch", [EG, P, TILES], I32, kind="Internal").ap()
    carry_d = nc.dram_tensor("carry_scratch", [3, EG + 1], F32, kind="Internal").ap()

    ctx = ExitStack()
    with ctx:
        def sb(name, shape, dt=F32):
            return ctx.enter_context(nc.sbuf_tensor(name, shape, dt))

        def sem(name):
            return ctx.enter_context(nc.semaphore(name))

        def sems(prefix, names):
            return {n: sem(f"{prefix}_{n}") for n in names.split()}

        def slot_sems(name, n):
            return [sem(f"{name}{k}") for k in range(n)]

        ident = sb("ident", [P, P])
        eps = sb("eps", [P, 1])
        free_b = sb("free_b", [P, 3, P])
        gamma_b, beta_b, b2b_b = (free_b[:, k, :] for k in range(3))
        msg_W1s = sb("msg_W1s", [P, 3, P])
        msg_W2s = sb("msg_W2s", [P, 1, P])
        upd_W1s = sb("upd_W1s", [P, 2, P])
        upd_W2s = sb("upd_W2s", [P, 1, P])
        W1as = sb("W1as", [P, 2, 2 * P])
        W1bs = sb("W1bs", [P, 2, P])
        W2as = sb("W2as", [P, 3, 2 * P])
        W2bs = sb("W2bs", [P, 2, P])
        cols = sb("cols", [P, 9])
        MSG_B1, MSG_B2, UPD_B1, B1A, B1B, B2A, GLOB = 0, 1, 2, 3, 5, 6, 8
        b2a_full = sb("b2a_full", [P, 2])
        ones3 = sb("ones3", [3, P], BF16)
        bias_f = sb("bias_f", [1, 2, P])
        bias_rest = sb("bias_rest", [1, 2, 2, P])
        bias_parts = sb("bias_parts", [1, 3, 2, GROUP], BF16)
        bias_rows = sb("bias_rows", [3, 2, GROUP], BF16)
        UPD_B2, B2B = 0, 1
        msg_W2T = sb("msg_W2T", [P, P])
        msg_upd_W = sb("msg_upd_W", [P, 1, P])
        msg_upd_f = sb("msg_upd_f", [1, 3, P])
        msg_upd_parts = sb("msg_upd_parts", [1, 3, P], BF16)
        msg_upd_rows = sb("msg_upd_rows", [6, P], BF16)
        dstc = sb("dstc", [P, EG, TILES], I32)
        nextc = sb("nextc", [P, EG, TILES], I32)
        samec = sb("samec", [P, EG, TILES])
        rowidx = sb("rowidx", [P, EG, TILES], I32)
        edge_row = sb("edge_row", [P, EG, TILES], I32)
        own_row = sb("own_row", [P, MAP_COLS], I32)
        ends = sb("ends", [1, 2, EG])
        carries = sb("carries", [1, EG + 1])
        carry_in = sb("carry_in", [EG, 1])

        big = [P, GROUP]
        n_taken = [0]
        room = [sb(f"room{k}", big) for k in range(63)]

        def take(n):
            n_taken[0] += n
            return room[n_taken[0] - n:n_taken[0]]

        dstr, prevr = (sb(w, [EG, GROUP], I32)[:, :] for w in ("dstr", "prevr"))
        samer, ones_r, zeros_r, count, through, count2, count3, rcount = (
            sb(w, [EG, GROUP])[:, :] for w in ("samer", "ones_r", "zeros_r", "count", "through", "count2", "count3", "rcount"))
        counts_hi, counts_lo = (sb(w, [EG, GROUP], BF16)[:, :] for w in ("counts_hi", "counts_lo"))

        n_x, n_xn, n_x1 = take(4), take(4), take(8)
        n_out, n_x1n = take(2), take(2)
        n_t, n_that, n_scaled, n_xb = take(2), take(2), take(2), take(4)
        n_hT, n_uT, n_h1T, n_v0T, n_v1T = take(2), take(2), take(2), take(2), take(2)
        a_xs, a_xd, a_xsn, a_xdn, a_xb = take(2), take(2), take(1), take(2), take(2)
        a_attrT, a_sT, a_dT = take(2), take(1), take(2)
        a_mT, a_sum, a_uT = take(1), take(2), take(1)
        a_t, a_that, a_scaled, a_new, a_same = take(1), take(1), take(1), take(1), take(1)
        n_taken[0] = 0
        b_xs, b_xd, b_xb, b_new = take(4), take(4), take(4), take(4)
        b_xsn, b_xdn, b_attrT, b_sT, b_dT = take(2), take(2), take(2), take(2), take(2)
        b_mT, b_uT = [take(2), take(2)], [take(2), take(2)]
        b_zT, b_sum, b_agg, b_same, b_rcount = take(2), take(2), take(2), take(2), take(2)

        a_counts = sb("a_counts", [6, GROUP], BF16)
        srcidx = [sb(f"srcidx_{k}", [P, TILES], I32) for k in range(4)]
        dstidx = [sb(f"dstidx_{k}", [P, TILES], I32) for k in range(2)]
        outidx = [sb(f"outidx_{k}", [P, TILES], I32) for k in range(4)]
        map_idx = [sb(f"map_idx_{k}", [P, TILES], I32) for k in range(2)]
        map_rows = [sb(f"map_rows_{k}", [P, TILES], I32) for k in range(2)]

        class Norms:

            def __init__(self, name):
                def two(what, *shape):
                    return [sb(f"{name}_{what}{k}", [P, 12, *shape]) for k in range(2)]
                self.stats = two("stats", 6)
                self.both, self.diff, self.sq = two("both"), two("diff"), two("sq")
                self.mean, self.sumsq, self.sd, self.rstd, self.shift = (
                    two("mean"), two("sumsq"), two("sd"), two("rstd"), two("shift"))

        node_norms, edge_norms = Norms("nn"), Norms("en")

        bank = [ctx.enter_context(nc.psum_tensor(f"bank{k}", big, F32)) for k in range(8)]
        hT_ps, v0_ps, v1_ps, o_ps, d_ps = bank[0:5]
        a_ps = bank[5:8]

        weights_in, bias_cols_in, edge_lists_in, bias_rows_in = map(
            sem, ("weights_in", "bias_cols_in", "edge_lists_in", "bias_rows_in"))
        ident_ready, const_ready, bias_chain, b2a_ready = map(sem, ("ident_ready", "const_ready", "bias_chain", "b2a_ready"))
        L = sems("lists", "idx idx_out count ends_out ends_in carry carry_out carry_in rcount rcount_out")
        W = sems("folded", "pe dve rows_in")
        N = sems("n", "stats link var sd norms xn hT_ps hT u_ps uT d_ps t that scaled xb x1 "
                      "x1n h1T_ps h1T v0_ps v1_ps v0T v1T o_ps out")
        n_x_in, n_x1_stored, n_out_stored = slot_sems("n_x_in", 4), slot_sems("n_x1_stored", 8), slot_sems("n_out_stored", 2)
        A = sems("a", "stats t_stats link var sd norms xsn xdn s_ps d_ps sT dT m_ps mT sum u_ps uT o_ps xb t that scaled new")
        a_idx_in, a_xs_in, a_xd_in, a_attr_in = (slot_sems(f"a_{w}_in", 2) for w in ("idx", "xs", "xd", "attr"))
        a_same_in, a_stored = slot_sems("a_same_in", 1), slot_sems("a_stored", 1)
        a_counts_in = sem("a_counts_in")
        map_own_in = sem("map_own_in")
        map_set_in, map_set, map_get_in, map_got, map_stored = (
            slot_sems(f"map_{w}", 2) for w in ("set_in", "set", "get_in", "got", "stored"))
        B = sems("b", "stats link var sd norms xsn xdn s_ps d_ps sT dT m_ps mT z_ps zT sum agg u_ps uT o_ps xb new")
        b_src_in, b_scattered, b_outidx_in = (slot_sems(f"b_{w}", 4) for w in ("src_in", "scattered", "outidx_in"))
        b_idx_in, b_xd_in, b_attr_in, b_same_in = (slot_sems(f"b_{w}_in", n) for w, n in (("idx", 4), ("xd", 4), ("attr", 2), ("same", 2)))

        N_WEIGHT_DMAS = 9
        N_COL_DMAS = 2

        MAP_TURNS = -(-EG // 4)
        A_STEPS = (-8, max(NG + 9, 4 * (EG + 2), 8 * MAP_TURNS + 2 * (EG + 1)))
        A_LOOP = (2, min((NG - 4) // 8, (EG - 2) // 2))
        SET_STEPS, SET_LOOP = (0, 8 * MAP_TURNS), (2, min(A_LOOP[1], (EG - 1) // 4))
        GET_STEPS, GET_LOOP = (8 * MAP_TURNS, A_STEPS[1]), (MAP_TURNS + 1, min(A_LOOP[1], MAP_TURNS + (EG - 1) // 4))
        B_STEPS, B_LOOP = (-4, EG + 3), (1, (EG - 4) // 4)

        def all_landed(eng, slots, groups, dmas=1):
            for k, s in enumerate(slots):
                eng.wait_ge(s, 16 * dmas * len(range(k, groups, len(slots))))

        def first_phase_done(eng):
            eng.wait_ge(N["out"], NG)
            eng.wait_ge(A["new"], EG)
            all_landed(eng, n_x1_stored, NG)
            all_landed(eng, n_out_stored, NG)
            all_landed(eng, a_stored, EG)

        def wait_all(eng, pairs):
            for _, count_ in pairs:
                if not isinstance(count_, int):
                    eng.lower_val(count_)
            eng.wait_ge(ident_ready, 2)
            for semaphore, count_ in pairs:
                eng.wait_ge(semaphore, count_)

        NO_LOOP = (0, 0)

        def map_group(i):
            return At(i.turn, i.slot // 2, 4)

        def last_group(g):
            return isinstance(g.turn, int) and g.index == NG - 1

        def node_rows(t, g):
            rows = t[n_nodes - GROUP:n_nodes, :] if last_group(g) else t[bass.ds(g.index * GROUP, GROUP), :]
            return rows.rearrange("(p j) f -> p (j f)", p=P)

        def edge_rows(t, g):
            return t[bass.ds(g.index * GROUP, GROUP), :].rearrange("(j p) f -> p j f", p=P)

        def tiles(t):
            return t[:, :].rearrange("p (j f) -> p j f", j=TILES)

        def tile(t, j):
            return t[:, j * P:(j + 1) * P]

        def list_row(t, g):
            return t[bass.ds(g.index, 1), :].broadcast_to([P, GROUP])

        def idx_cols(t, g):
            return t[bass.ds(g.index, 1), :, :].rearrange("o p j -> (o p) j")

        block = ctx.enter_context(nc.Block())

        @block.sync
        def _(sp):
            def list_loads():
                sp.dma_start(cols[:, :], bias_columns).then_inc(bias_cols_in, 16)
                sp.dma_start(bias_f[:, :, :], bias_rows_f.rearrange("(o b) f -> o b f", o=1)).then_inc(bias_cols_in, 16)
                sp.dma_start(dstc[:, :, :], dst_cols.rearrange("g p j -> p g j")).then_inc(edge_lists_in, 16)
                sp.dma_start(nextc[:, :, :], next_cols.rearrange("g p j -> p g j")).then_inc(edge_lists_in, 16)
                sp.dma_start(dstr, dst_rows).then_inc(edge_lists_in, 16)
                sp.dma_start(prevr, prev_rows).then_inc(edge_lists_in, 16)

            def list_stores(i):
                if i == -1:
                    sp.wait_ge(bias_chain, 8)
                    for k in range(3):
                        sp.dma_start(bias_rows[k:k + 1, :, :], bias_parts[:, k, :, :]).then_inc(bias_rows_in, 16)
                if i == 0:
                    sp.wait_ge(L["idx"], 3)
                    sp.dma_start(rowidx_d.rearrange("g p j -> p g j"), rowidx[:, :, :]).then_inc(L["idx_out"], 16)
                    sp.dma_start(same_d, samer).then_inc(L["idx_out"], 16)
                    sp.wait_ge(ident_ready, 4)
                    sp.dma_start(row_map.rearrange("(p c) o -> p (c o)", p=P), own_row[:, :]).then_inc(map_own_in, 16)
                    sp.dma_start(edge_row_d.rearrange("g p j -> p g j"), edge_row[:, :, :]).then_inc(L["idx_out"], 16)
                    sp.wait_ge(L["idx_out"], 48)
                    sp.wait_ge(L["count"], 2)
                    sp.dma_start(carry_d[0:1, 0:EG].rearrange("o g -> g o"), count[:, GROUP - 1:GROUP]).then_inc(L["ends_out"], 16)
                    sp.dma_start(carry_d[1:2, 0:EG].rearrange("o g -> g o"), through[:, GROUP - 1:GROUP]).then_inc(L["ends_out"], 16)
                    sp.wait_ge(L["ends_out"], 32)
                    sp.dma_start(ends[:, 0, :], carry_d[0:1, 0:EG]).then_inc(L["ends_in"], 16)
                    sp.dma_start(ends[:, 1, :], carry_d[1:2, 0:EG]).then_inc(L["ends_in"], 16)
                if i == 2:
                    sp.wait_ge(L["carry"], 2)
                    sp.dma_start(carry_d[2:3, :], carries[:, :]).then_inc(L["carry_out"], 16)
                    sp.wait_ge(L["carry_out"], 16)
                    sp.dma_start(carry_in[:, :], carry_d[2:3, 0:EG].rearrange("o g -> g o")).then_inc(L["carry_in"], 16)
                    sp.wait_ge(W["dve"], 8)
                    for k in range(6):
                        sp.dma_start(msg_upd_rows[k:k + 1, :], msg_upd_parts[:, k % 3, :]).then_inc(W["rows_in"], 16)
                if i == 4:
                    sp.wait_ge(L["rcount"], 3)
                    sp.dma_start(counts_d[0], counts_hi).then_inc(L["idx_out"], 16)
                    sp.dma_start(counts_d[1], counts_lo).then_inc(L["idx_out"], 16)
                    sp.wait_ge(L["idx_out"], 80)
                if i == 6:
                    sp.wait_ge(L["rcount"], 5)
                    sp.dma_start(rcount_d, rcount).then_inc(L["rcount_out"], 16)

            def step(i):
                g = i + 3
                if g.inside(NG):
                    if (g + -4).inside(NG):
                        sp.wait_ge(N["xb"], (g + -4).done)
                        sp.wait_ge(N["xn"], (g + -4).done)
                    sp.dma_start(n_x[g.ring(4)][:, :], node_rows(x, g)).then_inc(n_x_in[g.ring(4)], 16)
                if isinstance(i.turn, int):
                    list_stores(i.index)
                q, e = i.quarter()
                f = e + 2
                if q == 0 and f.inside(EG):
                    r = f.ring(2)
                    if (f + -2).inside(EG):
                        sp.wait_ge(a_xs_in[r], ring_landed(f + -2, 2, TILES))
                        sp.wait_ge(a_xd_in[r], ring_landed(f + -2, 2, TILES))
                    sp.dma_start(srcidx[r][:, :], idx_cols(src_cols, f)).then_inc(a_idx_in[r], 16)
                    sp.dma_start(dstidx[r][:, :], idx_cols(dst_cols, f)).then_inc(a_idx_in[r], 16)
                f = e
                if q == 1 and f.inside(EG):
                    if (f + -1).inside(EG):
                        sp.wait_ge(A["sum"], (f + -1).done)
                    sp.dma_start(a_same[0][:, :], list_row(same_d, f)).then_inc(a_same_in[0], 16)
                f = e + -1
                if q == 0 and f.inside(EG):
                    if (f + -1).inside(EG):
                        wait_all(sp, [(A["u_ps"], (f + -1).done)])
                    for part in range(2):
                        sp.dma_start(a_counts[3 * part:3 * part + 3, :],
                                     counts_d[part][bass.ds(f.index, 1), :].broadcast_to([3, GROUP])).then_inc(a_counts_in, 16)
                f = e + -2
                if q == 2 and f.inside(EG):
                    sp.wait_ge(A["new"], f.done)
                    sp.dma_start(edge_rows(x1_edge, f), tiles(a_new[0])).then_inc(a_stored[0], 16)
                f = e + 1
                if q == 3 and f.inside(EG):
                    r = f.ring(2)
                    if (f + -2).inside(EG):
                        sp.wait_ge(A["m_ps"], (f + -2).done)
                    sp.dma_start(a_attrT[r][:, :], edge_attr_T[:, bass.ds(f.index * GROUP, GROUP)]).then_inc(a_attr_in[r], 16)
                g = i + -3
                if g.inside(NG):
                    sp.wait_ge(N["x1"], g.done)
                    if last_group(g):
                        p = g + -1
                        sp.wait_ge(n_x1_stored[p.ring(8)], ring_landed(p, 8))
                    sp.dma_start(node_rows(x1, g), n_x1[g.ring(8)][:, :]).then_inc(n_x1_stored[g.ring(8)], 16)
                g = i + -8
                if g.inside(NG):
                    sp.wait_ge(N["out"], g.done)
                    if last_group(g):
                        p = g + -1
                        sp.wait_ge(n_out_stored[p.ring(2)], ring_landed(p, 2))
                    sp.dma_start(node_rows(out, g), n_out[g.ring(2)][:, :]).then_inc(n_out_stored[g.ring(2)], 16)

            def map_set_loads(m):
                r = m.ring(2)
                if (m + -2).inside(EG):
                    wait_all(sp, [(map_set[r], ring_landed(m + -2, 2, TILES))])
                sp.dma_start(map_idx[r][:, :], idx_cols(rowidx_d, m)).then_inc(map_set_in[r], 16)
                sp.dma_start(map_rows[r][:, :], idx_cols(edge_row_d, m)).then_inc(map_set_in[r], 16)

            def map_set_step(i):
                step(i)
                m = map_group(i)
                if isinstance(m.turn, int) and m.index == 0 and i.slot == 0:
                    map_set_loads(m)
                if i.slot % 2 == 0 and (m + 1).inside(EG):
                    map_set_loads(m + 1)

            def map_get_step(i):
                step(i)
                m = map_group(i) + (1 - 4 * MAP_TURNS)
                if i.slot % 2 == 0 and m.inside(EG):
                    r = m.ring(2)
                    if (m + -2).inside(EG):
                        wait_all(sp, [(map_got[r], ring_landed(m + -2, 2, TILES))])
                    sp.dma_start(map_idx[r][:, :], idx_cols(src_cols, m)).then_inc(map_get_in[r], 16)
                m = map_group(i) + (-1 - 4 * MAP_TURNS)
                if i.slot % 2 == 0 and m.inside(EG):
                    r = m.ring(2)
                    wait_all(sp, [(map_got[r], ring_landed(m, 2, TILES))])
                    sp.dma_start(idx_cols(src_row_d, m), map_rows[r][:, :]).then_inc(map_stored[r], 16)

            steps(sp, step, A_STEPS[0], -2, NO_LOOP, 8)
            list_loads()
            steps(sp, step, -2, SET_STEPS[0], NO_LOOP, 8)
            steps(sp, map_set_step, *SET_STEPS, SET_LOOP, 8)
            all_landed(sp, map_set, EG, TILES)
            sp.dma_start(map_idx[0][:, :], idx_cols(src_cols, At.number(0, 4))).then_inc(map_get_in[0], 16)
            steps(sp, map_get_step, *GET_STEPS, GET_LOOP, 8)
            all_landed(sp, map_stored, EG)
            sp.wait_ge(L["rcount_out"], 16)

            def edge_step(i):
                g = i + 4
                if g.inside(EG):
                    r = g.ring(4)
                    if (g + -4).inside(EG):
                        sp.wait_ge(b_src_in[r], ring_landed(g + -4, 4, TILES))
                    sp.dma_start(srcidx[r][:, :], idx_cols(src_row_d, g)).then_inc(b_idx_in[r], 16)
                g = i + 3
                if g.inside(EG):
                    r = g.ring(4)
                    if (g + -4).inside(EG):
                        sp.wait_ge(B["xb"], (g + -4).done)
                        sp.wait_ge(B["xdn"], (g + -4).done)
                    sp.dma_start(tiles(b_xd[r]), edge_rows(x1_edge, g)).then_inc(b_xd_in[r], 16)
                g = i + 1
                if g.inside(EG):
                    r = g.ring(2)
                    if (g + -2).inside(EG):
                        wait_all(sp, [(B["m_ps"], (g + -2).done)])
                    sp.dma_start(b_attrT[r][:, :], edge_attr_T[:, bass.ds(g.index * GROUP, GROUP)]).then_inc(b_attr_in[r], 16)
                g = i
                if g.inside(EG):
                    r = g.ring(2)
                    if (g + -2).inside(EG):
                        wait_all(sp, [(B["agg"], (g + -2).done)])
                    sp.dma_start(b_same[r][:, :], list_row(same_d, g)).then_inc(b_same_in[r], 16)
                    sp.dma_start(b_rcount[r][:, :], list_row(rcount_d, g)).then_inc(b_same_in[r], 16)
                    r = g.ring(4)
                    if (g + -4).inside(EG):
                        sp.wait_ge(b_scattered[r], ring_landed(g + -4, 4, TILES))
                    sp.dma_start(outidx[r][:, :], idx_cols(rowidx_d, g)).then_inc(b_outidx_in[r], 16)

            all_landed(sp, a_xs_in, EG, TILES)
            steps(sp, edge_step, B_STEPS[0], B_STEPS[0] + 1, NO_LOOP, 4)
            first_phase_done(sp)
            steps(sp, edge_step, B_STEPS[0] + 1, B_STEPS[1], B_LOOP, 4)
            all_landed(sp, b_scattered, EG, TILES)

        @block.tensor
        def _(pe):
            def transpose4(ps, src):
                for j in range(TILES):
                    last = pe.transpose(tile(ps, j), tile(src, j), ident[:, :])
                return last

            def product(ps, weights, h, parts):
                for k, (row, part) in enumerate(parts):
                    last = pe.matmul(ps[:, :], weights[:, row, h * P:(h + 1) * P], part[:, :],
                                     start=(k == 0), stop=(k == len(parts) - 1))
                return last

            def rows_product(ps, bias, parts, weights):
                if bias is not None:
                    pe.matmul(ps[:, :], ones3[:, :], bias_rows[:, bias, :], start=True, stop=False)
                for j in range(TILES):
                    for h, part in enumerate(parts):
                        last_of = h == len(parts) - 1
                        last = pe.matmul(tile(ps, j), tile(part, j), weights[:, h, :], start=(bias is None and h == 0),
                                         stop=(last_of and (bias is None or j == TILES - 1)))
                return last

            pe.wait_ge(ident_ready, 2)

            def step(i):
                q, e = i.quarter()
                g = i + -6
                if g.inside(NG):
                    pe.wait_ge(N["h1T"], g.done)
                    product(v0_ps, W2as, 0, [(0, n_h1T[g.ring(2)])]).then_inc(N["v0_ps"], 1)
                    product(v1_ps, W2as, 1, [(0, n_h1T[g.ring(2)])]).then_inc(N["v1_ps"], 1)
                f = e + -1
                if q == 1 and f.inside(EG):
                    if isinstance(f.turn, int) and f.index == 0:
                        pe.wait_ge(W["dve"], 3)
                        pe.wait_ge(W["rows_in"], 96)
                    pe.wait_ge(A["sum"], f.done)
                    pe.wait_ge(a_counts_in, ring_landed(f, 1, 2))
                    if (f + -1).inside(EG):
                        pe.wait_ge(A["t"], (f + -1).done)
                    pe.matmul(a_ps[2][:, :], msg_upd_rows[:, :], a_counts[:, :], start=True, stop=False)
                    pe.matmul(a_ps[2][:, :], upd_W1s[:, 0, :], a_dT[f.ring(2)][:, :], start=False, stop=False)
                    pe.matmul(a_ps[2][:, :], msg_upd_W[:, 0, :], a_sum[f.ring(2)][:, :], start=False, stop=True
                              ).then_inc(A["u_ps"], 1)
                if q == 3 and f.inside(EG):
                    pe.wait_ge(A["uT"], f.done)
                    rows_product(a_ps[2], UPD_B2, [a_uT[0]], upd_W2s).then_inc(A["o_ps"], 1)
                g = i + -5
                if g.inside(NG):
                    pe.wait_ge(N["x1n"], g.done)
                    pe.wait_ge(N["hT"], (i + 0).done if i.inside(NG) else NG)
                    transpose4(hT_ps, n_x1n[g.ring(2)]).then_inc(N["h1T_ps"], 1)
                g = i
                if g.inside(NG):
                    pe.wait_ge(N["hT"], g.done)
                    if (g + -6).inside(NG):
                        pe.wait_ge(N["v0T"], (g + -6).done)
                    product(v0_ps, upd_W1s, 0, [(0, n_hT[g.ring(2)])]).then_inc(N["u_ps"], 1)
                g = i + -6
                if g.inside(NG):
                    if (g + -1).inside(NG):
                        pe.wait_ge(N["out"], (g + -1).done)
                    pe.wait_ge(N["v0T"], g.done)
                    pe.wait_ge(N["v1T"], g.done)
                    rows_product(o_ps, B2B, [n_v0T[g.ring(2)], n_v1T[g.ring(2)]], W2bs).then_inc(N["o_ps"], 1)
                f = e
                if q == 2 and f.inside(EG):
                    pe.wait_ge(A["sT"], f.done)
                    pe.wait_ge(A["dT"], f.done)
                    pe.wait_ge(a_attr_in[f.ring(2)], ring_landed(f, 2))
                    product(a_ps[0], msg_W1s, 0, [(0, a_sT[0]), (1, a_dT[f.ring(2)]), (2, a_attrT[f.ring(2)])]
                            ).then_inc(A["m_ps"], 1)
                g = i + 1
                if g.inside(NG):
                    pe.wait_ge(N["xn"], g.done)
                    if (i + -5).inside(NG):
                        pe.wait_ge(N["h1T"], (i + -5).done)
                    transpose4(hT_ps, n_xn[g.ring(4)]).then_inc(N["hT_ps"], 1)
                g = i
                if g.inside(NG):
                    if (g + -1).inside(NG):
                        pe.wait_ge(N["t"], (g + -1).done)
                    pe.wait_ge(N["uT"], g.done)
                    rows_product(d_ps, UPD_B2, [n_uT[g.ring(2)]], upd_W2s).then_inc(N["d_ps"], 1)
                f = e
                if q == 1 and f.inside(EG):
                    pe.wait_ge(A["xsn"], f.done)
                    if (f + -1).inside(EG):
                        pe.wait_ge(A["mT"], (f + -1).done)
                    transpose4(a_ps[0], a_xsn[0]).then_inc(A["s_ps"], 1)
                    pe.wait_ge(A["xdn"], f.done)
                    transpose4(a_ps[1], a_xdn[f.ring(2)]).then_inc(A["d_ps"], 1)

            steps(pe, step, A_STEPS[0], 0, NO_LOOP, 8)
            pe.wait_ge(weights_in, 16 * N_WEIGHT_DMAS)
            pe.wait_ge(bias_cols_in, 16 * N_COL_DMAS)
            pe.transpose(bank[7][:, P:2 * P], msg_W2s[:, 0, :], ident[:, :])
            for h in range(2):
                last = pe.matmul(bank[7][:, h:h + 1], W2as[:, 2, h * P:(h + 1) * P], cols[:, GLOB:GLOB + 1],
                                 start=True, stop=True)
            last.then_inc(W["pe"], 1)
            pe.wait_ge(const_ready, 5)
            pe.wait_ge(bias_rows_in, 48)
            pe.wait_ge(b2a_ready, 1)
            steps(pe, step, 0, 1, NO_LOOP, 8)
            pe.wait_ge(W["dve"], 1)
            pe.matmul(bank[7][:, 2 * P:3 * P], msg_W2T[:, :], upd_W1s[:, 1, :], start=True, stop=True)
            pe.matmul(bank[7][0:1, 3 * P:4 * P], cols[:, MSG_B2:MSG_B2 + 1], upd_W1s[:, 1, :], start=True, stop=True
                      ).then_inc(W["pe"], 1)
            steps(pe, step, 1, A_STEPS[1], A_LOOP, 8)

            def edge_step(i):
                ta_ps, tb_ps, z_ps, d_ps = bank[0:4]
                m_ps, u_ps = bank[4:6], bank[6:8]
                g = i
                if g.inside(EG):
                    r = g.ring(2)
                    pe.wait_ge(B["sT"], g.done)
                    pe.wait_ge(b_attr_in[r], ring_landed(g, 2))
                    product(m_ps[0], W1as, 0, [(0, b_sT[r]), (1, b_attrT[r])])
                    product(m_ps[1], W1as, 1, [(0, b_sT[r]), (1, b_attrT[r])]).then_inc(B["m_ps"], 1)
                g = i + -1
                if g.inside(EG):
                    r = g.ring(2)
                    pe.wait_ge(B["dT"], g.done)
                    pe.wait_ge(B["agg"], g.done)
                    product(u_ps[0], W2as, 0, [(0, b_dT[r]), (1, b_agg[r])])
                    product(u_ps[1], W2as, 1, [(0, b_dT[r]), (1, b_agg[r])]).then_inc(B["u_ps"], 1)
                g = i
                if g.inside(EG):
                    r = g.ring(2)
                    pe.wait_ge(B["mT"], g.done)
                    product(z_ps, W1bs, 0, [(0, b_mT[0][r]), (1, b_mT[1][r])]).then_inc(B["z_ps"], 1)
                g = i + 1
                if g.inside(EG):
                    r = g.ring(2)
                    pe.wait_ge(B["xsn"], g.done)
                    transpose4(ta_ps, b_xsn[r]).then_inc(B["s_ps"], 1)
                    pe.wait_ge(B["xdn"], g.done)
                    transpose4(tb_ps, b_xdn[r]).then_inc(B["d_ps"], 1)
                g = i + -1
                if g.inside(EG):
                    r = g.ring(2)
                    if (g + -1).inside(EG):
                        pe.wait_ge(B["new"], (g + -1).done)
                    pe.wait_ge(B["uT"], g.done)
                    rows_product(d_ps, None, [b_uT[0][r], b_uT[1][r]], W2bs).then_inc(B["o_ps"], 1)

            first_phase_done(pe)
            steps(pe, edge_step, *B_STEPS, B_LOOP, 4)

        @block.scalar
        def _(act):
            def relu(out_, in_, bias=None):
                if bias is None:
                    return act.activation(out_[:, :], in_[:, :], ACT.Relu)
                return act.activation(out_[:, :], in_[:, :], ACT.Relu, bias=bias)

            def col(k):
                return cols[:, k:k + 1]

            def root(norms, r):
                return act.activation(norms.sd[r][:, :], norms.sumsq[r][:, :], ACT.Sqrt, bias=eps[:, :], scale=1.0 / D)

            def norm(norms, r, stream, dst, src):
                for j in range(TILES):
                    c = stream * TILES + j
                    last = act.activation(tile(dst, j), tile(src, j), ACT.Identity,
                                          bias=norms.shift[r][:, c:c + 1], scale=norms.rstd[r][:, c:c + 1])
                return last

            act.dma_start(free_b[:, :, :], free_rows.rearrange("(o k) f -> o k f", o=1).broadcast_to([P, 3, P])
                          ).then_inc(weights_in, 16)
            for dst, src in ((upd_W1s, upd_W1), (upd_W2s, upd_W2), (W2as, W2a), (W2bs, W2b),
                             (msg_W1s, msg_W1), (msg_W2s, msg_W2), (W1as, W1a), (W1bs, W1b)):
                act.dma_start(dst[:, :, :], src.rearrange("(k p) n -> p k n", p=P)).then_inc(weights_in, 16)
            act.wait_ge(const_ready, 5)

            def step(i):
                q, e = i.quarter()
                g = i + -6
                if g.inside(NG):
                    act.wait_ge(N["v0_ps"], g.done)
                    relu(n_v0T[g.ring(2)], v0_ps, b2a_full[:, 0:1]).then_inc(N["v0T"], 1)
                    act.wait_ge(N["v1_ps"], g.done)
                    relu(n_v1T[g.ring(2)], v1_ps, b2a_full[:, 1:2]).then_inc(N["v1T"], 1)
                f = e + -1
                if q == 1 and f.inside(EG):
                    act.wait_ge(A["u_ps"], f.done)
                    relu(a_uT[0], a_ps[2], col(UPD_B1)).then_inc(A["uT"], 1)
                g = i + -5
                if g.inside(NG):
                    act.wait_ge(N["h1T_ps"], g.done)
                    relu(n_h1T[g.ring(2)], hT_ps).then_inc(N["h1T"], 1)
                g = i
                if g.inside(NG):
                    act.wait_ge(N["u_ps"], g.done)
                    relu(n_uT[g.ring(2)], v0_ps, col(UPD_B1)).then_inc(N["uT"], 1)
                b = i + 1
                if b.inside(NG + 5):
                    act.wait_ge(N["norms"], b.done)
                g = i + -2
                if g.inside(NG):
                    if (g + -2).inside(NG):
                        act.wait_ge(N["scaled"], (g + -2).done)
                    norm(node_norms, b.ring(2), 1, n_that[g.ring(2)], n_t[g.ring(2)]).then_inc(N["that"], 1)
                g = i + -4
                if g.inside(NG):
                    if (g + -2).inside(NG):
                        act.wait_ge(N["h1T_ps"], (g + -2).done)
                    norm(node_norms, b.ring(2), 2, n_x1n[g.ring(2)], n_x1[g.ring(8)]).then_inc(N["x1n"], 1)
                b = i + 2
                if b.inside(NG + 5):
                    act.wait_ge(N["var"], b.done)
                    root(node_norms, b.ring(2)).then_inc(N["sd"], 1)
                g = i + 1
                if g.inside(NG):
                    act.wait_ge(N["hT_ps"], g.done)
                    relu(n_hT[g.ring(2)], hT_ps).then_inc(N["hT"], 1)
                f = e
                if q == 2 and f.inside(EG):
                    act.wait_ge(A["m_ps"], f.done)
                    if (f + -1).inside(EG):
                        act.wait_ge(A["sum"], (f + -1).done)
                    relu(a_mT[0], a_ps[0], col(MSG_B1)).then_inc(A["mT"], 1)
                f = e + -2
                if q == 0 and f.inside(EG):
                    act.wait_ge(A["norms"], e.done)
                    if (f + -1).inside(EG):
                        act.wait_ge(A["scaled"], (f + -1).done)
                    norm(edge_norms, e.ring(2), 2, a_that[0], a_t[0]).then_inc(A["that"], 1)
                b = e + 1
                if q == 3 and b.inside(EG + 2):
                    act.wait_ge(A["var"], b.done)
                    root(edge_norms, b.ring(2)).then_inc(A["sd"], 1)
                f = e
                if q == 1 and f.inside(EG):
                    act.wait_ge(A["s_ps"], f.done)
                    relu(a_sT[0], a_ps[0]).then_inc(A["sT"], 1)
                    act.wait_ge(A["d_ps"], f.done)
                    relu(a_dT[f.ring(2)], a_ps[1]).then_inc(A["dT"], 1)

            steps(act, step, A_STEPS[0], 0, NO_LOOP, 8)
            act.wait_ge(bias_cols_in, 16 * N_COL_DMAS)
            act.wait_ge(b2a_ready, 1)
            steps(act, step, 0, A_STEPS[1], A_LOOP, 8)

            def edge_step(i):
                ta_ps, tb_ps, z_ps, d_ps = bank[0:4]
                m_ps, u_ps = bank[4:6], bank[6:8]
                g = i
                if g.inside(EG):
                    r = g.ring(2)
                    act.wait_ge(B["m_ps"], g.done)
                    relu(b_mT[0][r], m_ps[0], col(B1A))
                    relu(b_mT[1][r], m_ps[1], col(B1A + 1)).then_inc(B["mT"], 1)
                g = i + -1
                if g.inside(EG):
                    r = g.ring(2)
                    act.wait_ge(B["u_ps"], g.done)
                    relu(b_uT[0][r], u_ps[0], b2a_full[:, 0:1])
                    relu(b_uT[1][r], u_ps[1], b2a_full[:, 1:2]).then_inc(B["uT"], 1)
                g = i
                if g.inside(EG):
                    r = g.ring(2)
                    act.wait_ge(B["z_ps"], g.done)
                    if (g + -2).inside(EG):
                        act.wait_ge(B["sum"], (g + -2).done)
                    act.activation(b_zT[r][:, :], z_ps[:, :], ACT.Identity, bias=col(B1B)).then_inc(B["zT"], 1)
                g = i + 1
                if g.inside(EG):
                    r = g.ring(2)
                    act.wait_ge(B["s_ps"], g.done)
                    relu(b_sT[r], ta_ps).then_inc(B["sT"], 1)
                    act.wait_ge(B["d_ps"], g.done)
                    relu(b_dT[r], tb_ps).then_inc(B["dT"], 1)
                g = i + 2
                if g.inside(EG):
                    act.wait_ge(B["var"], g.done)
                    root(edge_norms, g.ring(2)).then_inc(B["sd"], 1)

            first_phase_done(act)
            steps(act, edge_step, *B_STEPS, B_LOOP, 4)

        @block.vector
        def _(dve):
            def stats(norms, r, stream, src):
                for j in range(TILES):
                    last = dve.bn_stats(norms.stats[r][:, stream * TILES + j, :], tile(src, j))
                return last

            def variances(norms, r, link, n):
                s = norms.stats[r]
                dve.tensor_tensor(norms.diff[r][:, :], s[:, :, 1], s[:, :, 4], ALU.subtract).then_inc(link, 1)
                dve.tensor_tensor(norms.both[r][:, :], s[:, :, 2], s[:, :, 5], ALU.add)
                dve.wait_ge(link, 3 * n - 2)
                dve.scalar_tensor_tensor(out=norms.sq[r][:, :], in0=norms.diff[r][:, :], scalar=D / 4.0,
                                         in1=norms.diff[r][:, :], op0=ALU.mult, op1=ALU.mult).then_inc(link, 1)
                dve.scalar_tensor_tensor(out=norms.mean[r][:, :], in0=norms.diff[r][:, :], scalar=-0.5, in1=s[:, :, 1],
                                         op0=ALU.mult, op1=ALU.add)
                dve.wait_ge(link, 3 * n - 1)
                return dve.tensor_tensor(norms.sumsq[r][:, :], norms.sq[r][:, :], norms.both[r][:, :], ALU.add)

            def invert(norms, r, link, n):
                dve.reciprocal(norms.rstd[r][:, :], norms.sd[r][:, :]).then_inc(link, 1)
                dve.wait_ge(link, 3 * n)
                return dve.scalar_tensor_tensor(out=norms.shift[r][:, :], in0=norms.mean[r][:, :], scalar=-1.0,
                                                in1=norms.rstd[r][:, :], op0=ALU.mult, op1=ALU.mult)

            def norm(norms, r, stream, dst, src):
                for j in range(TILES):
                    c = stream * TILES + j
                    last = dve.tensor_scalar(tile(dst, j), tile(src, j), norms.mean[r][:, c:c + 1],
                                             norms.rstd[r][:, c:c + 1], ALU.subtract, ALU.mult)
                return last

            for norms in (node_norms, edge_norms):
                for r in range(2):
                    dve.memset(norms.stats[r][:, :, :], 0.0).then_inc(const_ready, 1)
            dve.memset(eps[:, :], LN_EPS)
            dve.memset(ones3[:, :], 1.0)
            dve.memset(ones_r, 1.0)
            dve.memset(carries[:, :], 0.0)
            dve.memset(zeros_r, 0.0).then_inc(const_ready, 1)
            dve.wait_ge(const_ready, 5)

            def edge_counts(i):
                if i == 1:
                    dve.wait_ge(L["ends_in"], 32)
                    dve.tensor_tensor_scan(carries[:, 1:EG + 1], ends[:, 1, :], ends[:, 0, :], 0.0, ALU.mult, ALU.add
                                           ).then_inc(L["carry"], 2)
                    dve.wait_ge(W["pe"], 2)
                    dve.tensor_copy(msg_upd_W[:, 0, :], bank[7][:, 2 * P:3 * P]).then_inc(W["dve"], 1)
                    dve.tensor_copy(msg_upd_f[:, 0, :], bank[7][0:1, 3 * P:4 * P]).then_inc(W["dve"], 1)
                    dve.wait_ge(W["dve"], 3)
                    for k in range(3):
                        dve.tensor_copy(msg_upd_parts[:, k, :], msg_upd_f[:, k, :]).then_inc(W["dve"], 1)
                        if k < 2:
                            dve.wait_ge(W["dve"], 2 * k + 4)
                            dve.tensor_tensor(msg_upd_f[:, k + 1, :], msg_upd_f[:, k, :], msg_upd_parts[:, k, :],
                                              ALU.subtract).then_inc(W["dve"], 1)
                            dve.wait_ge(W["dve"], 2 * k + 5)
                if i == 3:
                    dve.wait_ge(L["carry_in"], 16)
                    dve.scalar_tensor_tensor(out=count2, in0=through, scalar=carry_in[:, 0:1], in1=count,
                                             op0=ALU.mult, op1=ALU.add).then_inc(L["rcount"], 1)
                    dve.wait_ge(L["rcount"], 1)
                    dve.tensor_copy(counts_hi, count2).then_inc(L["rcount"], 1)
                    dve.wait_ge(L["rcount"], 2)
                    dve.tensor_tensor(counts_lo, count2, counts_hi, ALU.subtract).then_inc(L["rcount"], 1)
                if i == 5:
                    dve.tensor_scalar(count3, count2, 1.0, None, ALU.max).then_inc(L["rcount"], 1)
                    dve.wait_ge(L["rcount"], 4)
                    dve.reciprocal(rcount, count3).then_inc(L["rcount"], 1)

            def step(i):
                q, e = i.quarter()
                b = i + 1
                if b.inside(NG + 5):
                    dve.wait_ge(N["sd"], b.done)
                    invert(node_norms, b.ring(2), N["link"], b.done).then_inc(N["norms"], 1)
                g = i + 1
                if g.inside(NG):
                    norm(node_norms, b.ring(2), 0, n_xn[g.ring(4)], n_x[g.ring(4)]).then_inc(N["xn"], 1)
                if q == 0 and e.inside(EG + 2):
                    dve.wait_ge(A["sd"], e.done)
                    invert(edge_norms, e.ring(2), A["link"], e.done).then_inc(A["norms"], 1)
                if q == 1 and e.inside(EG):
                    if (e + -1).inside(EG):
                        dve.wait_ge(A["s_ps"], (e + -1).done)
                    norm(edge_norms, e.ring(2), 0, a_xsn[0], a_xs[e.ring(2)]).then_inc(A["xsn"], 1)
                    norm(edge_norms, e.ring(2), 1, a_xdn[e.ring(2)], a_xd[e.ring(2)]).then_inc(A["xdn"], 1)
                g = i + -7
                if g.inside(NG):
                    dve.wait_ge(N["o_ps"], g.done)
                    if (g + -2).inside(NG):
                        dve.wait_ge(n_out_stored[g.ring(2)], ring_landed(g + -2, 2))
                    dve.tensor_tensor(n_out[g.ring(2)][:, :], o_ps[:, :], n_x1[g.ring(8)][:, :], ALU.add
                                      ).then_inc(N["out"], 1)
                g = i + -1
                if g.inside(NG):
                    dve.wait_ge(N["d_ps"], g.done)
                    if (g + -2).inside(NG):
                        dve.wait_ge(N["that"], (g + -2).done)
                    dve.scalar_tensor_tensor(out=n_t[g.ring(2)][:, :], in0=n_xn[g.ring(4)][:, :], scalar=0.0,
                                             in1=d_ps[:, :], op0=ALU.max, op1=ALU.add).then_inc(N["t"], 1)
                f = e + -1
                if q == 0 and f.inside(EG):
                    dve.wait_ge(a_same_in[0], ring_landed(f, 1))
                    dve.wait_ge(A["mT"], f.done)
                    before = 0.0
                    if (f + -1).inside(EG):
                        dve.wait_ge(A["sum"], (f + -1).done)
                        before = a_sum[(f + -1).ring(2)][:, GROUP - 1:GROUP]
                    dve.tensor_tensor_scan(a_sum[f.ring(2)][:, :], a_same[0][:, :], a_mT[0][:, :], before,
                                           ALU.mult, ALU.add).then_inc(A["sum"], 1)
                b = i + 2
                r = b.ring(2)
                g, last = b, None
                if g.inside(NG):
                    dve.wait_ge(n_x_in[g.ring(4)], ring_landed(g, 4))
                    last = stats(node_norms, r, 0, n_x[g.ring(4)])
                g = i + -3
                if g.inside(NG):
                    dve.wait_ge(N["x1"], g.done)
                    last = stats(node_norms, r, 2, n_x1[g.ring(8)])
                g = i + -1
                if g.inside(NG):
                    dve.wait_ge(N["t"], g.done)
                    last = stats(node_norms, r, 1, n_t[g.ring(2)])
                if b.inside(NG + 5):
                    last.then_inc(N["stats"], 1)
                    dve.wait_ge(N["stats"], b.done)
                    variances(node_norms, r, N["link"], b.done).then_inc(N["var"], 1)
                eb = e + 1
                if q == 2 and eb.inside(EG):
                    dve.wait_ge(a_xs_in[eb.ring(2)], ring_landed(eb, 2, TILES))
                    stats(edge_norms, eb.ring(2), 0, a_xs[eb.ring(2)])
                    dve.wait_ge(a_xd_in[eb.ring(2)], ring_landed(eb, 2, TILES))
                    stats(edge_norms, eb.ring(2), 1, a_xd[eb.ring(2)]).then_inc(A["stats"], 1)
                f = e + -1
                if q == 3 and f.inside(EG):
                    dve.wait_ge(A["o_ps"], f.done)
                    dve.scalar_tensor_tensor(out=a_t[0][:, :], in0=a_xdn[f.ring(2)][:, :], scalar=0.0,
                                             in1=a_ps[2][:, :], op0=ALU.max, op1=ALU.add).then_inc(A["t"], 1)
                if q == 3 and eb.inside(EG + 2):
                    if f.inside(EG):
                        dve.wait_ge(A["t"], f.done)
                        stats(edge_norms, eb.ring(2), 2, a_t[0]).then_inc(A["t_stats"], 1)
                        dve.wait_ge(A["t_stats"], f.done)
                    if eb.inside(EG):
                        dve.wait_ge(A["stats"], eb.done)
                    variances(edge_norms, eb.ring(2), A["link"], eb.done).then_inc(A["var"], 1)
                g = i
                if g.inside(NG):
                    if (g + -4).inside(NG):
                        dve.wait_ge(N["x1"], (g + -4).done)
                    dve.tensor_tensor(tiles(n_xb[g.ring(4)]), tiles(n_x[g.ring(4)]), beta_b.unsqueeze(1).broadcast_to([P, TILES, P]),
                                      ALU.add).then_inc(N["xb"], 1)
                if isinstance(i.turn, int):
                    edge_counts(i.index)

            steps(dve, step, A_STEPS[0], -2, NO_LOOP, 8)
            dve.wait_ge(bias_cols_in, 16 * N_COL_DMAS)

            def wide(k):
                return bias_parts[:, k, :, :].rearrange("o b (j f) -> o b j f", j=TILES)

            rests = [bias_f[:, :, :], bias_rest[:, 0, :, :], bias_rest[:, 1, :, :]]
            n = 0
            for k in range(3):
                for b in range(2):
                    dve.tensor_copy(wide(k)[:, b, :, :],
                                    rests[k][:, b, :].unsqueeze(1).broadcast_to([1, TILES, P])).then_inc(bias_chain, 1)
                n += 2
                dve.wait_ge(bias_chain, n)
                if k < 2:
                    dve.tensor_tensor(rests[k + 1], rests[k], wide(k)[:, :, 0, :], ALU.subtract).then_inc(bias_chain, 1)
                    n += 1
                    dve.wait_ge(bias_chain, n)
            steps(dve, step, -2, 0, NO_LOOP, 8)
            dve.wait_ge(W["pe"], 1)
            dve.tensor_tensor(b2a_full[:, :], bank[7][:, 0:2], cols[:, B2A:B2A + 2], ALU.add).then_inc(b2a_ready, 1)
            dve.wait_ge(edge_lists_in, 64)
            dve.tensor_tensor(samec[:, :, :], dstc[:, :, :], nextc[:, :, :], ALU.is_equal).then_inc(L["idx"], 1)
            dve.wait_ge(L["idx"], 1)
            dve.scalar_tensor_tensor(out=rowidx[:, :, :], in0=samec[:, :, :], scalar=float(NO_ROW), in1=dstc[:, :, :],
                                     op0=ALU.mult, op1=ALU.add).then_inc(L["idx"], 1)
            dve.tensor_tensor(samer, dstr, prevr, ALU.is_equal).then_inc(L["idx"], 1)
            dve.wait_ge(L["idx"], 3)
            dve.tensor_tensor_scan(count, samer, ones_r, 0.0, ALU.mult, ALU.add).then_inc(L["count"], 1)
            dve.tensor_tensor_scan(through, samer, zeros_r, 1.0, ALU.mult, ALU.add).then_inc(L["count"], 1)
            dve.tensor_copy(msg_W2T[:, :], bank[7][:, P:2 * P]).then_inc(W["dve"], 1)
            dve.wait_ge(weights_in, 16 * N_WEIGHT_DMAS)
            steps(dve, step, 0, A_STEPS[1], A_LOOP, 8)

            def edge_step(i):
                d_ps = bank[3]
                g = i + -1
                if g.inside(EG):
                    r = g.ring(2)
                    dve.wait_ge(b_same_in[r], ring_landed(g, 2, 2))
                    dve.wait_ge(B["zT"], g.done)
                    before = 0.0
                    if (g + -1).inside(EG):
                        dve.wait_ge(B["sum"], (g + -1).done)
                        before = b_sum[1 - r][:, GROUP - 1:GROUP]
                    dve.tensor_tensor_scan(b_sum[r][:, :], b_same[r][:, :], b_zT[r][:, :], before, ALU.mult, ALU.add
                                           ).then_inc(B["sum"], 1)
                    dve.wait_ge(B["sum"], g.done)
                    dve.tensor_tensor(b_agg[r][:, :], b_sum[r][:, :], b_rcount[r][:, :], ALU.mult).then_inc(B["agg"], 1)
                g = i + 1
                if g.inside(EG):
                    dve.wait_ge(B["sd"], g.done)
                    r = g.ring(2)
                    invert(edge_norms, r, B["link"], g.done).then_inc(B["norms"], 1)
                    norm(edge_norms, r, 0, b_xsn[r], b_xs[g.ring(4)]).then_inc(B["xsn"], 1)
                    norm(edge_norms, r, 1, b_xdn[r], b_xd[g.ring(4)]).then_inc(B["xdn"], 1)
                g = i + 2
                if g.inside(EG):
                    r = g.ring(2)
                    dve.wait_ge(b_src_in[g.ring(4)], ring_landed(g, 4, TILES))
                    stats(edge_norms, r, 0, b_xs[g.ring(4)])
                    dve.wait_ge(b_xd_in[g.ring(4)], ring_landed(g, 4))
                    stats(edge_norms, r, 1, b_xd[g.ring(4)]).then_inc(B["stats"], 1)
                    dve.wait_ge(B["stats"], g.done)
                    variances(edge_norms, r, B["link"], g.done).then_inc(B["var"], 1)
                g = i + -2
                if g.inside(EG):
                    dve.wait_ge(B["o_ps"], g.done)
                    dve.wait_ge(B["xb"], g.done)
                    if (g + -4).inside(EG):
                        dve.wait_ge(b_scattered[g.ring(4)], ring_landed(g + -4, 4, TILES))
                    dve.tensor_tensor(b_new[g.ring(4)][:, :], d_ps[:, :], b_xb[g.ring(4)][:, :], ALU.add
                                      ).then_inc(B["new"], 1)

            first_phase_done(dve)
            steps(dve, edge_step, *B_STEPS, B_LOOP, 4)

        @block.gpsimd
        def _(pool):
            pool.memset(ident[:, :], 0.0).then_inc(ident_ready, 1)
            pool.wait_ge(ident_ready, 1)
            pool.affine_select(out=ident[:, :], in_=ident[:, :], compare_op=ALU.not_equal, fill=1.0, base=0,
                               pattern=[[-1, P]], channel_multiplier=1).then_inc(ident_ready, 1)
            pool.iota(own_row[:, :], pattern=[[1, MAP_COLS]], base=0, channel_multiplier=MAP_COLS).then_inc(ident_ready, 1)
            pool.iota(edge_row[:, :, :], pattern=[[GROUP, EG], [P, TILES]], base=n_nodes, channel_multiplier=1
                      ).then_inc(ident_ready, 1)

            def over_tiles(dst, src, row, op):
                return pool.tensor_tensor(tiles(dst), tiles(src), row.unsqueeze(1).broadcast_to([P, TILES, P]), op)

            def gather(dst, table, idx, j, semaphore):
                pool.indirect_dma_start(out=tile(dst, j), out_offset=None, in_=table,
                                        in_offset=bass.IndirectOffsetOnAxis(ap=idx[:, j:j + 1], axis=0)
                                        ).then_inc(semaphore, 16)

            def scatter(table, idx, src, semaphore):
                for j in range(TILES):
                    pool.indirect_dma_start(out=table, in_=tile(src, j), in_offset=None,
                                            out_offset=bass.IndirectOffsetOnAxis(ap=idx[:, j:j + 1], axis=0),
                                            bounds_check=n_nodes - 1, oob_is_err=False).then_inc(semaphore, 16)

            def step(i):
                q, e = i.quarter()
                g = i + -2
                if g.inside(NG):
                    s = g.ring(2)
                    pool.wait_ge(N["that"], g.done)
                    over_tiles(n_scaled[s], n_that[s], gamma_b, ALU.mult).then_inc(N["scaled"], 1)
                    pool.wait_ge(N["scaled"], g.done)
                    if (g + -8).inside(NG):
                        pool.wait_ge(N["out"], (g + -8).done)
                        pool.wait_ge(n_x1_stored[g.ring(8)], ring_landed(g + -8, 8))
                    pool.wait_ge(N["xb"], g.done)
                    pool.tensor_tensor(n_x1[g.ring(8)][:, :], n_scaled[s][:, :], n_xb[g.ring(4)][:, :], ALU.add
                                       ).then_inc(N["x1"], 1)
                f = e + 2 if q else e + 1
                r = f.ring(2)
                if f.inside(EG):
                    first = q in (1, 3)
                    if first:
                        waits = [(a_idx_in[r], ring_landed(f, 2, 2))]
                        if (f + -2).inside(EG):
                            waits.append((A["xsn" if q == 1 else "xdn"], (f + -2).done))
                            if q == 3:
                                waits.append((A["xb"], (f + -2).done))
                        wait_all(pool, waits)
                    for j in ((0, 1) if first else (2, 3)):
                        if q in (1, 2):
                            gather(a_xs[r], x, srcidx[r], j, a_xs_in[r])
                        else:
                            gather(a_xd[r], x, dstidx[r], j, a_xd_in[r])
                if q == 2 and e.inside(EG):
                    pool.wait_ge(a_xd_in[e.ring(2)], ring_landed(e, 2, TILES))
                    if (e + -2).inside(EG):
                        pool.wait_ge(A["new"], (e + -2).done)
                    over_tiles(a_xb[e.ring(2)], a_xd[e.ring(2)], beta_b, ALU.add).then_inc(A["xb"], 1)
                f = e + -2
                if q == 1 and f.inside(EG):
                    pool.wait_ge(A["that"], f.done)
                    if (f + -1).inside(EG):
                        pool.wait_ge(A["new"], (f + -1).done)
                    over_tiles(a_scaled[0], a_that[0], gamma_b, ALU.mult).then_inc(A["scaled"], 1)
                    pool.wait_ge(A["scaled"], f.done)
                    if (f + -1).inside(EG):
                        pool.wait_ge(a_stored[0], ring_landed(f + -1, 1))
                    pool.tensor_tensor(a_new[0][:, :], a_scaled[0][:, :], a_xb[f.ring(2)][:, :], ALU.add
                                       ).then_inc(A["new"], 1)

            def map_set_step(i):
                m = map_group(i)
                r, half = m.ring(2), i.slot % 2
                if m.inside(EG):
                    if half == 0:
                        wait_all(pool, [(map_set_in[r], ring_landed(m, 2, 2))])
                    for j in (2 * half, 2 * half + 1):
                        pool.indirect_dma_start(out=row_map, in_=map_rows[r][:, j:j + 1], in_offset=None,
                                                out_offset=bass.IndirectOffsetOnAxis(ap=map_idx[r][:, j:j + 1], axis=0),
                                                bounds_check=n_nodes - 1, oob_is_err=False).then_inc(map_set[r], 16)
                step(i)

            def map_get_step(i):
                m = map_group(i) + -4 * MAP_TURNS
                r, half = m.ring(2), i.slot % 2
                if m.inside(EG):
                    if half == 0:
                        waits = [(map_get_in[r], ring_landed(m, 2))]
                        if (m + -2).inside(EG):
                            waits.append((map_stored[r], ring_landed(m + -2, 2)))
                        wait_all(pool, waits)
                    for j in (2 * half, 2 * half + 1):
                        pool.indirect_dma_start(out=map_rows[r][:, j:j + 1], out_offset=None, in_=row_map,
                                                in_offset=bass.IndirectOffsetOnAxis(ap=map_idx[r][:, j:j + 1], axis=0)
                                                ).then_inc(map_got[r], 16)
                step(i)

            steps(pool, step, A_STEPS[0], 0, NO_LOOP, 8)
            pool.wait_ge(weights_in, 16 * N_WEIGHT_DMAS)
            pool.wait_ge(map_own_in, 16)
            steps(pool, map_set_step, *SET_STEPS, SET_LOOP, 8)
            all_landed(pool, map_set, EG, TILES)
            steps(pool, map_get_step, *GET_STEPS, GET_LOOP, 8)
            first_phase_done(pool)

            def edge_step(i):
                g = i + 3
                if g.inside(EG):
                    r = g.ring(4)
                    waits = [(b_idx_in[r], ring_landed(g, 4))]
                    if (g + -4).inside(EG):
                        waits.append((B["xsn"], (g + -4).done))
                    wait_all(pool, waits)
                    for j in range(TILES):
                        gather(b_xs[r], x1_table, srcidx[r], j, b_src_in[r])
                g = i + 1
                if g.inside(EG):
                    r = g.ring(4)
                    pool.wait_ge(b_xd_in[r], ring_landed(g, 4))
                    if (g + -4).inside(EG):
                        pool.wait_ge(B["new"], (g + -4).done)
                    over_tiles(b_xb[r], b_xd[r], b2b_b, ALU.add).then_inc(B["xb"], 1)
                g = i + -3
                if g.inside(EG):
                    r = g.ring(4)
                    wait_all(pool, [(B["new"], g.done), (b_outidx_in[r], ring_landed(g, 4))])
                    scatter(out, outidx[r], b_new[r], b_scattered[r])

            steps(pool, edge_step, *B_STEPS, B_LOOP, 4)


def kernel(**inputs):
    import numpy as np
    import concourse.bacc as bacc
    from concourse.bass_utils import run_bass_kernel_spmd

    a = {k: np.ascontiguousarray(v) for k, v in inputs.items()}
    n_edges = a["src"].shape[0]
    groups = -(-n_edges // GROUP)
    pad = groups * GROUP - n_edges

    def padded(v, fill):
        return np.concatenate([v, np.full((pad,) + v.shape[1:], fill, v.dtype)])

    def columns(v):
        return np.ascontiguousarray(v.reshape(groups, TILES, P).transpose(0, 2, 1))

    dst, none = a["dst"], np.full(1, -1, a["dst"].dtype)
    arrays = {
        "x": a["x"],
        "edge_attr_T": np.ascontiguousarray(padded(a["edge_attr_128"], 0).T),
        "src_cols": columns(padded(a["src"], 0)),
        "dst_cols": columns(padded(dst, 0)),
        "next_cols": columns(padded(np.concatenate([dst[1:], none]), 0)),
        "dst_rows": padded(dst, -1).reshape(groups, GROUP),
        "prev_rows": padded(np.concatenate([none, dst[:-1]]), -2).reshape(groups, GROUP),
    }
    columns_of = [a["L0_gnn_msg_b1"], a["L0_gnn_msg_b2"], a["L0_gnn_upd_b1"], a["L1_gnn_b1a"], a["L1_gnn_b1b"],
                  a["L1_gnn_b2a"], a["L1_gnn_u"][0]]
    arrays["bias_columns"] = np.ascontiguousarray(np.concatenate([v.reshape(-1, P) for v in columns_of]).T)
    arrays["bias_rows_f"] = np.stack([a["L0_gnn_upd_b2"], a["L1_gnn_b2b"]])
    arrays["free_rows"] = np.stack([a["L0_gnn_ln_gamma"], a["L0_gnn_ln_beta"], a["L1_gnn_b2b"]])
    for k in ("msg_W1", "msg_W2", "upd_W1", "upd_W2"):
        arrays[k] = a["L0_gnn_" + k]
    for k in ("W1a", "W1b", "W2a", "W2b"):
        arrays[k] = a["L1_gnn_" + k]

    nc = bacc.Bacc("TRN2", target_bir_lowering=False, num_devices=1)
    aps = {k: nc.dram_tensor(k, v.shape, mybir.dt.from_np(v.dtype), kind="ExternalInput").ap() for k, v in arrays.items()}
    out = nc.dram_tensor("out", a["x"].shape, F32, kind="ExternalOutput").ap()
    build(nc, **aps, out=out)
    r = run_bass_kernel_spmd(nc, [arrays], core_ids=[0])
    return r.results[0]["out"]
```
